# Optimizing a Trainium2 kernel written in Bass

```python
import numpy as np
import jax
import jax.numpy as jnp

def _softmax(x, axis=-1):
    return jax.nn.softmax(x, axis=axis)

def _gelu(x):
    return jax.nn.gelu(x, approximate=True)

def _silu(x):
    return jax.nn.silu(x)

def _sigmoid(x):
    return jax.nn.sigmoid(x)

def _layernorm(x, axis=-1, eps=1e-05):
    m = jnp.mean(x, axis=axis, keepdims=True)
    v = jnp.var(x, axis=axis, keepdims=True)
    return (x - m) / jnp.sqrt(v + eps)

def _scatter_add(tgt, idx, src, axis=0):
    return tgt.at[idx].add(src)

def _segment_sum(src, seg, n):
    return jax.ops.segment_sum(src, seg, n)
kernel_name = 'mk_adj_ffn_d1_adj_r2_728968'

def setup_inputs(seed: int=0):
    np.random.seed(seed)
    _w = jnp.asarray

    def _rec_inputs():
        import jax
        import jax.numpy as jnp
        _gk = jax.random.key(seed)
        x = -0.0005207 + 1.001 * jax.random.normal(jax.random.fold_in(_gk, 1), (1354, 128), jnp.float32)
        _a = jax.random.bernoulli(jax.random.fold_in(_gk, 2), 0.00295421, (1354, 1354))
        _a = jnp.logical_or(_a, jnp.swapaxes(_a, -1, -2))
        _a = jnp.logical_or(_a, jnp.eye(1354, dtype=bool))
        _af = _a.astype(jnp.float32)
        _af = _af * jax.random.uniform(jax.random.fold_in(_gk, 3), (1354, 1354), jnp.float32, 0.05, 1)
        adj = _af
        return (x, adj)
    x, adj = _rec_inputs()

    def _L0_gnn_setup():
        import jax, jax.numpy as jnp
        import numpy as np
        D_IN = 128
        D_ATTN = 64
        STEPS = 2
        TOP_P = 0.9
        TAU = 1.0
        LN_EPS = 1e-05
        N_NODES = 4096

        def _top_p_attention(X, W1, W2, W3):
            q = X @ W1.T @ W2.T
            k = X @ W3.T
            logits = q @ k.T / TAU
            probs = jax.nn.softmax(logits, axis=-1)
            idx = jnp.argsort(-probs, axis=-1)
            sp = jnp.take_along_axis(probs, idx, axis=-1)
            cs = jnp.cumsum(sp, axis=-1)
            keep_sorted = cs - sp < TOP_P
            rows = jnp.arange(probs.shape[0])[:, None]
            mask = jnp.zeros(probs.shape, dtype=bool).at[rows, idx].set(keep_sorted)
            A = probs * mask
            return A / jnp.maximum(A.sum(-1, keepdims=True), 1e-12)
        key = jax.random.key(seed)
        ks = jax.random.split(key, 8)
        N, d, da, steps = (N_NODES, D_IN, D_ATTN, STEPS)
        X = jax.random.normal(ks[0], (N, d), dtype=jnp.float32)
        S = jax.random.uniform(ks[1], (N, N), dtype=jnp.float32)
        W1 = jax.random.normal(ks[2], (da, d), dtype=jnp.float32) / np.sqrt(d)
        W2 = jax.random.normal(ks[3], (da, da), dtype=jnp.float32) / np.sqrt(da)
        W3 = jax.random.normal(ks[4], (da, d), dtype=jnp.float32) / np.sqrt(d)
        U1 = jax.random.normal(ks[5], (steps, d, d), dtype=jnp.float32) / np.sqrt(d)
        U2 = jax.random.normal(ks[6], (steps, d, d), dtype=jnp.float32) / np.sqrt(d)
        ln_g = jnp.ones((d,), dtype=jnp.float32)
        ln_b = jnp.zeros((d,), dtype=jnp.float32)
        return {'X': X, 'S': S, 'W1': W1, 'W2': W2, 'W3': W3, 'U1': U1, 'U2': U2, 'ln_g': ln_g, 'ln_b': ln_b}
    _L0_gnn_all = _L0_gnn_setup()
    _L0_gnn_in = {k: v for k, v in _L0_gnn_all.items() if k in ('W1', 'W2', 'W3', 'U1', 'U2', 'ln_g', 'ln_b')}
    del _L0_gnn_all

    def _L0_ffn_setup():
        import jax, jax.numpy as jnp
        import numpy as np
        D_IN, D_HID, D_OUT = (128, 256, 128)
        N_EXPERTS, TOP_K = (64, 2)
        B, S = (8, 2048)
        key = jax.random.key(seed)
        ks = jax.random.split(key, 8)
        scale_in = 1.0 / np.sqrt(D_IN)
        scale_hid = 1.0 / np.sqrt(D_HID)
        return {'x': jax.random.normal(ks[0], (B, S, D_IN), dtype=jnp.float32), 'Wr': jax.random.uniform(ks[1], (D_IN, N_EXPERTS), jnp.float32, -scale_in, scale_in), 'br': jax.random.uniform(ks[2], (N_EXPERTS,), jnp.float32, -scale_in, scale_in), 'W1': jax.random.uniform(ks[3], (N_EXPERTS, D_IN, D_HID), jnp.float32, -scale_in, scale_in), 'b1': jax.random.uniform(ks[4], (N_EXPERTS, D_HID), jnp.float32, -scale_in, scale_in), 'W2': jax.random.uniform(ks[5], (N_EXPERTS, D_HID, D_OUT), jnp.float32, -scale_hid, scale_hid), 'b2': jax.random.uniform(ks[6], (N_EXPERTS, D_OUT), jnp.float32, -scale_hid, scale_hid)}
    _L0_ffn_all = _L0_ffn_setup()
    _L0_ffn_in = {k: v for k, v in _L0_ffn_all.items() if k in ('Wr', 'br', 'W1', 'b1', 'W2', 'b2')}
    del _L0_ffn_all
    return {'x': x, 'adj': adj, 'L0_gnn_W1': _L0_gnn_in['W1'], 'L0_gnn_W2': _L0_gnn_in['W2'], 'L0_gnn_W3': _L0_gnn_in['W3'], 'L0_gnn_U1': _L0_gnn_in['U1'], 'L0_gnn_U2': _L0_gnn_in['U2'], 'L0_gnn_ln_g': _L0_gnn_in['ln_g'], 'L0_gnn_ln_b': _L0_gnn_in['ln_b'], 'L0_ffn_Wr': _L0_ffn_in['Wr'], 'L0_ffn_br': _L0_ffn_in['br'], 'L0_ffn_W1': _L0_ffn_in['W1'], 'L0_ffn_b1': _L0_ffn_in['b1'], 'L0_ffn_W2': _L0_ffn_in['W2'], 'L0_ffn_b2': _L0_ffn_in['b2']}

def reference(x, adj, L0_gnn_W1, L0_gnn_W2, L0_gnn_W3, L0_gnn_U1, L0_gnn_U2, L0_gnn_ln_g, L0_gnn_ln_b, L0_ffn_Wr, L0_ffn_br, L0_ffn_W1, L0_ffn_b1, L0_ffn_W2, L0_ffn_b2):
    import jax
    import jax.numpy as jnp

    def _L0_gnn_ref(X, S, W1, W2, W3, U1, U2, ln_g, ln_b):
        import jax, jax.numpy as jnp
        import numpy as np
        D_IN = 128
        D_ATTN = 64
        STEPS = 2
        TOP_P = 0.9
        TAU = 1.0
        LN_EPS = 1e-05
        N_NODES = 4096

        def _top_p_attention(X, W1, W2, W3):
            q = X @ W1.T @ W2.T
            k = X @ W3.T
            logits = q @ k.T / TAU
            probs = jax.nn.softmax(logits, axis=-1)
            idx = jnp.argsort(-probs, axis=-1)
            sp = jnp.take_along_axis(probs, idx, axis=-1)
            cs = jnp.cumsum(sp, axis=-1)
            keep_sorted = cs - sp < TOP_P
            rows = jnp.arange(probs.shape[0])[:, None]
            mask = jnp.zeros(probs.shape, dtype=bool).at[rows, idx].set(keep_sorted)
            A = probs * mask
            return A / jnp.maximum(A.sum(-1, keepdims=True), 1e-12)
        N = X.shape[0]
        R = S + jnp.eye(N, dtype=X.dtype)
        R = R / R.sum(-1, keepdims=True)
        Z = jnp.zeros_like(X)
        Xf = X
        Xa = X
        for n in range(STEPS):
            A = _top_p_attention(Xa, W1, W2, W3)
            Xf = R @ Xf
            Xa = A @ Xa
            Z = Z + Xf @ U1[n].T + Xa @ U2[n].T
        h = X + Z
        mu = h.mean(-1, keepdims=True)
        var = jnp.mean((h - mu) ** 2, axis=-1, keepdims=True)
        return (h - mu) / jnp.sqrt(var + LN_EPS) * ln_g + ln_b

    def _L0_ffn_ref(x, Wr, br, W1, b1, W2, b2):
        import jax, jax.numpy as jnp
        import numpy as np
        D_IN, D_HID, D_OUT = (128, 256, 128)
        N_EXPERTS, TOP_K = (64, 2)
        B, S = (8, 2048)
        Bx, Sx, D = x.shape
        xf = x.reshape(-1, D)
        T = xf.shape[0]
        E = Wr.shape[1]
        logits = xf @ Wr + br
        topk_logits, topk_idx = jax.lax.top_k(logits, TOP_K)
        gates = jax.nn.softmax(topk_logits, axis=1)
        combine = jnp.zeros((T, E), xf.dtype).at[jnp.arange(T)[:, None], topk_idx].add(gates)
        out = jnp.zeros((T, W2.shape[-1]), xf.dtype)
        for e in range(E):
            h = jax.nn.relu(xf @ W1[e] + b1[e])
            y = h @ W2[e] + b2[e]
            out = out + combine[:, e:e + 1] * y
        return out.reshape(Bx, Sx, -1)
    x = x + _L0_gnn_ref(_layernorm(x, axis=-1), adj, L0_gnn_W1, L0_gnn_W2, L0_gnn_W3, L0_gnn_U1, L0_gnn_U2, L0_gnn_ln_g, L0_gnn_ln_b)
    x = x + _L0_ffn_ref(_layernorm(x, axis=-1)[None], L0_ffn_Wr, L0_ffn_br, L0_ffn_W1, L0_ffn_b1, L0_ffn_W2, L0_ffn_b2)[0]
    return x

_drawn_inputs = setup_inputs


def setup_inputs(seed=0):
    import zlib

    import numpy as np

    out = dict(_drawn_inputs(seed))
    spreads = {'L0_gnn_ln_g': (1.0, 0.2), 'L0_gnn_ln_b': (0.0, 0.1)}
    factors = {'L0_ffn_b1': 7.003, 'L0_ffn_b2': 4.055}
    for name, (base, spread) in spreads.items():
        noise = np.random.default_rng([zlib.crc32(name.encode()), seed]).standard_normal(out[name].shape)
        drawn = base * np.exp(spread * noise) if base else spread * noise
        out[name] = jnp.asarray(drawn.astype(out[name].dtype))
    for name, factor in factors.items():
        out[name] = (out[name] * factor).astype(out[name].dtype)
    return out
```

```python
import math
from contextlib import ExitStack

import concourse.bass as bass
from concourse import mybir

P = 128
N = 1354
D = 128
DA = 64
STEPS = 2
TOP_P = 0.9
EPS = 1e-5
T = -(-N // P)
NP = T * P
LAST = N - (T - 1) * P
E = 64
F = 256
FC = F // P
CAP = 96
ROUNDS = -(-N // CAP)
SLOTS = 16
GROUPS = E // SLOTS
WIDTH = (113, 35)
CHUNKS = tuple(-(-N // w) for w in WIDTH)
RANGE = math.log2(2 * N / (1.0 - TOP_P)) + 0.1
STEPS_OF_CUT = (6, 10)
RETRY = 6
PARTS = ((0, 6), (6, T))
EXACT = 32
FAR = float(E * CAP * 2)


def build(nc, x, adj_t, w1_t, w2_t, w3_t, u_t, ln_g, ln_b, wr, br, ew1, eb1, ew2, eb2, consts, out):
    BF16 = mybir.dt.bfloat16
    F32, I32, U32 = mybir.dt.float32, mybir.dt.int32, mybir.dt.uint32
    ALU = mybir.AluOpType
    ACT = mybir.ActivationFunctionType
    AX = mybir.AxisListType

    slot_x = nc.dram_tensor("slot_x", [E * CAP, D], F32, kind="Internal").ap()
    slot_y = nc.dram_tensor("slot_y", [E * CAP, D], F32, kind="Internal").ap()

    with ExitStack() as ctx:
        def sb(name, shape, dt=F32):
            return ctx.enter_context(nc.sbuf_tensor(name, shape, dt))

        def sem(name):
            return ctx.enter_context(nc.semaphore(name))

        adj = sb("adj", [P, T, NP])
        probs = sb("probs", [P, T, N])
        xraw = sb("xraw", [P, T, D])
        f0 = sb("f0", [P, T, D + 1])
        f1 = sb("f1", [P, T, D + 1])
        a1 = sb("a1", [P, T, D])
        t_a = sb("t_a", [P, NP])
        t_a2 = sb("t_a2", [P, NP])
        t_f1 = sb("t_f1", [P, NP])
        t_f2 = sb("t_f2", [P, NP])
        q_t = sb("q_t", [DA, NP])
        k_t = sb("k_t", [DA, NP])
        p_t = sb("p_t", [P, 2, T, P])
        below = t_a2[:, 0:N]
        cand = sb("cand", [P, T, 8 * max(CHUNKS)])
        picked = below[:, 0:2 * 8 * max(CHUNKS)].rearrange("p (b c) -> p b c", b=2)
        column = t_f2[:, 0:N // 2].bitcast(mybir.dt.int16)
        raised = t_f2[:, N // 2:N].bitcast(BF16)
        most_tiles = max(b - a for a, b in PARTS)
        junk = t_a2[:, :].bitcast(BF16)[:, 0:most_tiles * 8 * max(CHUNKS)].rearrange("p (t c) -> p t c", t=most_tiles)
        w1s = sb("w1s", [D, DA])
        w2s = sb("w2s", [DA, DA])
        w3s = sb("w3s", [D, DA])
        us = sb("us", [P, 2 * STEPS, D])
        wrs = sb("wrs", [D, E])
        brs = sb("brs", [P, E])
        cs = sb("cs", [P, 3 * P + E + 1])
        ident, tri, ones = cs[:, 0:P], cs[:, P:2 * P], cs[:, 2 * P:3 * P]
        iota = cs[:, 3 * P:3 * P + E]
        real = cs[:, 3 * P + E:3 * P + E + 1]
        stats = sb("stats", [P, T, 6])
        mv = sb("mv", [P, T, 2])
        rstd = sb("rstd", [P, T])
        etop = sb("etop", [P, T, 8])
        negmax = sb("negmax", [P, T])
        cum = sb("cum", [P, T, 9])
        done8 = sb("done8", [P, T, 8])
        work8 = sb("work8", [P, T, 8])
        zsum = sb("zsum", [P, T])
        target = sb("target", [P, T])
        lo = sb("lo", [P, T])
        hi = sb("hi", [P, T])
        mid = sb("mid", [P, T])
        mass = sb("mass", [P, T])
        above = sb("above", [P, T])
        found = sb("found", [P, T])
        hidden = sb("hidden", [P, T])
        ties = sb("ties", [P, T])
        one_i = sb("one_i", [P, T], I32)
        last7 = sb("last7", [P, T, 7])
        place = sb("place", [P, T, 8], U32)
        retop = sb("retop", [P, 1, 8])
        redone = sb("redone", [P, 1, 8])
        opened = sb("opened", [P, 1], U32)
        flag32 = sb("flag32", [P, 32])
        flag32t = sb("flag32t", [P, 32])
        low_i = sb("low_i", [P, T], I32)
        high_i = sb("high_i", [P, T], I32)
        yes = sb("yes", [P, T], U32)
        no = sb("no", [P, T], U32)
        cut = sb("cut", [P, T])
        flags = sb("flags", [P, T])
        flag1 = sb("flag1", [P, 1])
        flag_i = sb("flag_i", [P, 1], I32)
        kept = sb("kept", [P, T])
        rkept = sb("rkept", [P, T])
        rrow = sb("rrow", [P, T])
        rinv = sb("rinv", [P, T])

        flat_p = probs[:, :, :].rearrange("p t n -> p (t n)")
        xg = flat_p[0:CAP, 0:E * D].rearrange("p (e d) -> p e d", e=E)
        xgt = flat_p[:, E * D:E * D + E * CAP].rearrange("p (e c) -> p e c", e=E)
        late = flat_p[:, E * D + E * CAP:E * D + E * CAP + 4 * D].rearrange("p (k d) -> p k d", k=4)
        gs, bs, eb1s, eb2s = late[:, 0, :], late[:, 1, :], late[:, 2, :], late[0:E, 3, :]
        zero = flat_p[:, 0:E * CAP * D // P]
        flat_s = adj[:, :, :].rearrange("p t n -> p (t n)")
        at = 0

        def region(n):
            nonlocal at
            at += n
            return flat_s[:, at - n:at]

        rw1 = region(SLOTS * F).rearrange("p (s f) -> p s f", s=SLOTS)
        rw2 = region(SLOTS * FC * D).rearrange("p (s c d) -> p s c d", s=SLOTS, c=FC)
        ysb = region(SLOTS * D).rearrange("p (s d) -> p s d", s=SLOTS)
        yg = region(2 * T * D).rearrange("p (k t d) -> p k t d", k=2, t=T)
        hid = region(2 * FC * P).rearrange("p (b c n) -> p b c n", b=2, c=FC)
        assert at <= T * NP
        flat_pt = p_t[:, :, :, :].rearrange("p b t n -> p (b t n)")
        lg = flat_pt[:, 0:T * E].rearrange("p (t e) -> p t e", t=T)
        m1 = flat_pt[:, T * E:2 * T * E].rearrange("p (t e) -> p t e", t=T)
        m2 = flat_pt[:, 2 * T * E:3 * T * E].rearrange("p (t e) -> p t e", t=T)
        flat_f1 = f1[:, :, :].rearrange("p t n -> p (t n)")
        mm = flat_f1[:, 0:T * E].rearrange("p (t e) -> p t e", t=T)
        macc = flat_f1[:, T * E:2 * T * E].rearrange("p (t e) -> p t e", t=T)
        comb = flat_pt[:, 3 * T * E:4 * T * E].rearrange("p (t e) -> p t e", t=T)
        comb_t = k_t
        ranks = t_f1[:, 0:T * E].rearrange("p (t e) -> p t e", t=T)
        prod = t_f1[:, T * E:2 * T * E].rearrange("p (t e) -> p t e", t=T)
        hrow = a1
        xn = xraw_n = f0[:, :, 0:D]
        x1 = t_f2[:, :].rearrange("p (t d) -> p t d", t=T)
        tmp = t_a2[:, :].rearrange("p (t d) -> p t d", t=T)
        acc = a1
        flat_c = cand[:, :, :].rearrange("p t c -> p (t c)")
        used = 0

        def small(*shape, dt=F32):
            nonlocal used
            size = math.prod(shape)
            used += size
            piece = flat_c[:, used - size:used]
            piece = piece if dt is F32 else piece.bitcast(dt)
            return piece if len(shape) == 1 else piece.rearrange("p (a b) -> p a b", a=shape[0])

        top = small(T, 8)
        idx8 = small(T, 8, dt=U32)
        eidx = small(2, T)
        rank = small(2, T)
        base = small(2, T)
        ok1 = small(2, T)
        ok2 = small(2, T)
        slot = small(2, T)
        slot_i = small(2, T, dt=I32)
        gate = small(2, T)
        gdiff = small(T)
        gexp = small(T)
        most = small(1)
        most_i = small(1, dt=I32)

        psum = ctx.enter_context(nc.psum_tensor("psum", [P, 8, 512], F32))
        flat = psum[:, :, :].rearrange("p b n -> p (b n)")
        SETS = [flat[:, 0:1536], flat[:, 1536:3072]]

        s_x, s_adj, s_w, s_xr = sem("x_loaded"), sem("adj_loaded"), sem("weights_loaded"), sem("x_reloaded")
        s_zero, s_zeroed = sem("zero_tile_ready"), sem("slots_zeroed")
        s_col = sem("column_numbers_ready")
        s_var, s_std = sem("variance_ready"), sem("std_ready")
        s_norm = sem("rows_normalised")
        s_tp, s_te = sem("transposes_done"), sem("transposes_copied")
        s_proj, s_projc = sem("projections_done"), sem("projections_copied")
        s_lg = [sem(f"logits_ready{n}") for n in range(STEPS)]
        s_neg = [sem(f"negmax_ready{n}") for n in range(STEPS)]
        s_exp = [sem(f"exp_done{n}") for n in range(STEPS)]
        s_r = [sem(f"adj_product_ready{n}") for n in range(STEPS)]
        s_rc = [sem(f"adj_product_copied{n}") for n in range(STEPS)]
        s_rs = [sem(f"adj_product_scaled{n}") for n in range(STEPS)]
        s_mask = [sem(f"kept_ready{n}") for n in range(STEPS)]
        s_pt = [sem(f"kept_transposed{n}") for n in range(STEPS)]
        s_ptc = [sem(f"kept_transpose_copied{n}") for n in range(STEPS)]
        s_a = [sem(f"attention_ready{n}") for n in range(STEPS)]
        s_ac = [sem(f"attention_copied{n}") for n in range(STEPS)]
        s_h, s_hc = sem("h_ready"), sem("h_copied")
        s_rl, s_rlc = sem("router_logits_ready"), sem("router_logits_read")
        s_gd, s_ge = sem("gate_difference_ready"), sem("gate_exp_ready")
        s_m, s_rk, s_rkc = sem("choices_ready"), sem("ranks_ready"), sem("ranks_read")
        s_cb, s_cbt, s_cbtc, s_b2 = sem("combine_ready"), sem("combine_transposed"), sem("combine_copied"), sem("bias_ready")
        s_most = sem("largest_count_ready")
        s_slot, s_sent = sem("slots_ready"), sem("tokens_sent")
        s_xg = sem("tokens_loaded")
        s_wl = [sem(f"expert_weights{s}") for s in range(SLOTS)]
        s_pass = sem("wait_passed")
        s_xt, s_xtf = sem("tokens_transposed"), sem("transpose_banks_freed")
        s_hp, s_hf = sem("hidden_ready"), sem("hidden_banks_freed")
        s_y, s_yf = sem("expert_out_ready"), sem("out_banks_freed")
        s_ys, s_yg = sem("expert_out_stored"), sem("outputs_gathered")
        s_acc, s_out = sem("result_ready"), sem("result_stored")
        block = ctx.enter_context(nc.Block())

        chunks = [(0, 512), (512, 512), (1024, N - 1024)]
        wide = [(0, 512), (512, 512), (1024, NP - 1024)]

        def rows(c):
            return P if c < T - 1 else LAST

        def held(eng, semaphore, value):
            eng.wait_ge(semaphore, value)
            eng.sem_inc(s_pass, 1)

        def each_round(eng, body):
            body(0)
            eng.wait_ge(s_most, 1)
            largest = eng.value_load(most_i[0:1, 0:1], min_val=0, max_val=N)
            with eng.Fori(1, ROUNDS) as r:
                with eng.If(largest > r * CAP):
                    body(r)

        @block.sync
        def _(sp):
            sp.dma_start(xraw[:, :, :], x.rearrange("(t p) d -> p t d", p=P)).then_inc(s_x, 16)
            for dst, src in ((w1s, w1_t), (w2s, w2_t), (w3s, w3_t), (cs, consts),
                             (wrs, wr), (brs, br)):
                sp.dma_start(dst[:, :], src).then_inc(s_w, 16)
            sp.dma_start(us[:, :, :], u_t.rearrange("(u d) o -> d u o", d=D)).then_inc(s_w, 16)
            sp.dma_start(adj[:, 0:T - 1, :], adj_t[0:(T - 1) * P, :].rearrange("(t p) n -> p t n", p=P)).then_inc(s_adj, 16)
            sp.dma_start(adj[0:LAST, T - 1, :], adj_t[(T - 1) * P:N, :]).then_inc(s_adj, 16)
            sp.wait_ge(s_zero, 1)
            sp.dma_start(slot_x.rearrange("(p k) d -> p (k d)", p=P), zero).then_inc(s_zeroed, 16)
            sp.wait_ge(s_tp, 5)
            sp.dma_start(xraw[:, :, :], x.rearrange("(t p) d -> p t d", p=P)).then_inc(s_xr, 16)
            for dst, src in ((gs, ln_g), (bs, ln_b), (eb1s, eb1), (eb2s, eb2)):
                sp.dma_start(dst, src).then_inc(s_xr, 16)

            def body(r):
                def group(g):
                    for s in range(SLOTS):
                        e = g * SLOTS + s
                        sp.wait_ge(s_y, r * E + e + 1)
                        sp.dma_start(rw1[:, s, :], ew1[bass.ds(e * D, D), :]).then_inc(s_wl[s], 16)
                        sp.dma_start(rw2[:, s, :, :], ew2[bass.ds(e * F, F), :].rearrange("(c p) d -> p c d", p=P)).then_inc(s_wl[s], 16)
                with sp.Fori(0, GROUPS) as g:
                    group(g)
            each_round(sp, body)
            sp.wait_ge(s_acc, 1)
            sp.dma_start(out[0:(T - 1) * P, :].rearrange("(t p) d -> p t d", p=P), acc[:, 0:T - 1, :]).then_inc(s_out, 16)
            sp.dma_start(out[(T - 1) * P:N, :], acc[0:LAST, T - 1, :]).then_inc(s_out, 16)
            sp.wait_ge(s_out, 32)

        @block.gpsimd
        def _(gp):
            nc.gpsimd.memset(zero, 0.0).then_inc(s_zero, 1)
            gp.iota(column, pattern=[[1, N]], base=0, channel_multiplier=0, allow_small_or_imprecise_dtypes=True).then_inc(s_col, 1)
            gp.wait_ge(s_zeroed, 16)

            def body(r):
                held(gp, s_slot, r + 1)
                for k in range(2):
                    for i in range(T):
                        gp.indirect_dma_start(out=slot_x, out_offset=bass.IndirectOffsetOnAxis(ap=slot_i[:, k, i:i + 1], axis=0),
                                              in_=xn[:, i, :], in_offset=None, bounds_check=E * CAP - 1, oob_is_err=False).then_inc(s_sent, 16)
                held(gp, s_sent, (r + 1) * (2 * T * 16))
                for q in range(GROUPS):
                    gp.dma_start(xg[:, q * SLOTS:(q + 1) * SLOTS, :],
                                 slot_x[q * SLOTS * CAP:(q + 1) * SLOTS * CAP, :].rearrange("(e c) d -> c e d", c=CAP)).then_inc(s_xg, 16)
                held(gp, s_ys, (r + 1) * (GROUPS * 16) + 16)
                for k in range(2):
                    for i in range(T):
                        gp.indirect_dma_start(out=yg[:, k, i, :], out_offset=None, in_=slot_y,
                                              in_offset=bass.IndirectOffsetOnAxis(ap=slot_i[:, k, i:i + 1], axis=0),
                                              bounds_check=E * CAP - 1, oob_is_err=False).then_inc(s_yg, 16)
            each_round(gp, body)

        @block.tensor
        def _(pe):
            def transposes(src, which, width=D):
                for i in range(T):
                    last = nc.tensor.transpose(SETS[which][0:width, i * P:(i + 1) * P], src[:, i, 0:width], ident)
                last.then_inc(s_tp, 1)

            pe.wait_ge(s_w, 16 * 7)
            pe.wait_ge(s_norm, 1)
            transposes(f0, 0)
            for n in range(STEPS):
                ta = t_a
                pe.wait_ge(s_te, 1 if n == 0 else 3)
                for c0, w in wide:
                    last = nc.tensor.matmul(SETS[1][0:DA, c0:c0 + w], w1s[:, :], ta[:, c0:c0 + w], start=True, stop=True)
                last.then_inc(s_proj, 1)
                for c0, w in wide:
                    last = nc.tensor.matmul(SETS[0][0:DA, c0:c0 + w], w3s[:, :], ta[:, c0:c0 + w], start=True, stop=True)
                last.then_inc(s_proj, 1)
                pe.wait_ge(s_projc, 3 * n + 1)
                for c0, w in wide:
                    last = nc.tensor.matmul(SETS[1][0:DA, c0:c0 + w], w2s[:, :], p_t[0:DA, 0, :, :].rearrange("p t n -> p (t n)")[:, c0:c0 + w], start=True, stop=True)
                last.then_inc(s_proj, 1)
                pe.wait_ge(s_projc, 3 * n + 3)
                for i in range(T):
                    if i >= 2:
                        pe.wait_ge(s_exp[n], i - 1)
                    for c0, w in chunks:
                        last = nc.tensor.matmul(SETS[i % 2][:, c0:c0 + w], q_t[:, i * P:(i + 1) * P], k_t[:, c0:c0 + w], start=True, stop=True)
                    last.then_inc(s_lg[n], 1)
                pe.wait_ge(s_adj, 32)
                if n == 1:
                    pe.wait_ge(s_rs[0], 1)
                fin = f0 if n == 0 else f1
                for i in range(T):
                    if i >= 2:
                        pe.wait_ge(s_rc[n], i - 1)
                    ob = psum[:, 6 + i % 2, 0:D + 1]
                    for c in range(T):
                        nc.tensor.matmul(ob, adj[0:rows(c), c, i * P:(i + 1) * P], fin[0:rows(c), c, 0:D + 1], start=(c == 0), stop=False)
                    nc.tensor.matmul(ob, ident, fin[:, i, 0:D + 1], start=False, stop=True).then_inc(s_r[n], 1)
                pe.wait_ge(s_rc[n], T)
                pe.wait_ge(s_exp[n], T)
                vin = f0 if n == 0 else a1
                for i in range(T + 1):
                    if i < T:
                        pe.wait_ge(s_mask[n], i + 1)
                        if i >= 2:
                            pe.wait_ge(s_ptc[n], i - 1)
                        for c in range(T):
                            last = nc.tensor.transpose(SETS[i % 2][0:rows(c), c * P:(c + 1) * P], probs[:, i, c * P:c * P + rows(c)], ident)
                        last.then_inc(s_pt[n], 1)
                    if i >= 1:
                        j = i - 1
                        pe.wait_ge(s_ptc[n], j + 1)
                        if j >= 2:
                            pe.wait_ge(s_ac[n], j - 1)
                        for c in range(T):
                            last = nc.tensor.matmul(psum[:, 6 + j % 2, 0:D], p_t[0:rows(c), j % 2, c, :], vin[0:rows(c), c, 0:D], start=(c == 0), stop=(c == T - 1))
                        last.then_inc(s_a[n], 1)
                pe.wait_ge(s_ac[n], T)
                pe.wait_ge(s_rs[n], 1)
                if n == 0:
                    transposes(f1, 0)
                    transposes(a1, 1)
                    pe.wait_ge(s_te, 3)
                else:
                    transposes(f1, 1)
                    transposes(xraw, 0)
                    pe.wait_ge(s_te, 5)
            nc.tensor.drain().then_inc(s_y, SLOTS)
            for i in range(T):
                if i >= 2:
                    pe.wait_ge(s_hc, i - 1)
                ob = psum[:, 6 + i % 2, 0:D]
                for u, src in enumerate((t_f1, t_f2, t_a, t_a2)):
                    nc.tensor.matmul(ob, src[:, i * P:(i + 1) * P], us[:, u, :], start=(u == 0), stop=False)
                nc.tensor.matmul(ob, ident, f0[:, i, 0:D], start=False, stop=True).then_inc(s_h, 1)
            pe.wait_ge(s_norm, 2)
            transposes(xn, 0)
            pe.wait_ge(s_te, 6)
            for i in range(T):
                last = nc.tensor.matmul(SETS[1][:, i * E:(i + 1) * E], t_a[:, i * P:(i + 1) * P], wrs[:, :], start=True, stop=True, skip_group_check=True)
            last.then_inc(s_rl, 1)
            pe.wait_ge(s_m, 1)
            for i in range(T):
                ob = SETS[0][:, i * E:(i + 1) * E]
                nc.tensor.matmul(ob, tri, mm[:, i, :], start=True, stop=(i == 0))
                if i > 0:
                    nc.tensor.matmul(ob, ones, macc[:, i - 1, :], start=False, stop=True)
            nc.tensor.matmul(SETS[0][:, T * E:(T + 1) * E], ones, macc[:, T - 1, :], start=True, stop=True).then_inc(s_rk, 1)
            pe.wait_ge(s_cb, 1)
            pe.wait_ge(s_rlc, 1)
            for i in range(T):
                last = nc.tensor.transpose(SETS[1][0:E, i * P:(i + 1) * P], comb[:, i, :], ident)
            last.then_inc(s_cbt, 1)
            pe.wait_ge(s_cbtc, 1)
            pe.wait_ge(s_rkc, 1)
            for i in range(T):
                last = nc.tensor.matmul(SETS[0][:, i * D:(i + 1) * D], comb_t[:, i * P:(i + 1) * P], eb2s, start=True, stop=True)
            last.then_inc(s_b2, 1)

            def body(r):
                held(pe, s_xg, (r + 1) * (GROUPS * 16))
                for b in range(E // 4):
                    pe.wait_ge(s_xtf, r * (E // 4) + b + 1)
                    for k in range(4):
                        last = nc.tensor.transpose(psum[:, b % 2, k * CAP:(k + 1) * CAP], xg[:, 4 * b + k, :], ident[0:CAP, 0:CAP])
                    last.then_inc(s_xt, 1)
                held(pe, s_xtf, (r + 1) * (E // 4) + 2)

                def group(g):
                    for s in range(SLOTS + 1):
                        if s < SLOTS:
                            e = g * SLOTS + s
                            held(pe, s_wl[s], 32 * (r * GROUPS + g + 1))
                            pe.wait_ge(s_hf, r * E + e + 1)
                            for c in range(FC):
                                last = nc.tensor.matmul(psum[:, 2 + s % 2, c * CAP:(c + 1) * CAP], rw1[:, s, c * P:(c + 1) * P],
                                                        xgt[:, bass.ds(e, 1), :], start=True, stop=True)
                            last.then_inc(s_hp, 1)
                        if s >= 1:
                            e = g * SLOTS + s - 1
                            pe.wait_ge(s_hf, r * E + e + 3)
                            pe.wait_ge(s_yf, r * E + e + 1)
                            for c in range(FC):
                                last = nc.tensor.matmul(psum[0:CAP, 4 + (s - 1) % 2, 0:D], hid[:, (s - 1) % 2, c, 0:CAP], rw2[:, s - 1, c, :],
                                                        start=(c == 0), stop=(c == FC - 1))
                            last.then_inc(s_y, 1)
                with pe.Fori(0, GROUPS) as g:
                    group(g)
            each_round(pe, body)

        @block.scalar
        def _(act):
            def std(k):
                act.wait_ge(s_var, k)
                nc.scalar.activation(rstd[:, :], rstd[:, :], ACT.Sqrt).then_inc(s_std, 1)

            def copy_out(dst, which, k, width=D):
                act.wait_ge(s_tp, k)
                nc.scalar.activation(dst[0:width, :], SETS[which][0:width, 0:NP], ACT.Copy).then_inc(s_te, 1)

            std(1)
            copy_out(t_a, 0, 1)
            for n in range(STEPS):
                tmid = p_t[0:DA, 0, :, :].rearrange("p t n -> p (t n)")
                for k, (dst, which) in enumerate(((tmid, 1), (k_t[:, :], 0), (q_t[:, :], 1))):
                    act.wait_ge(s_proj, 3 * n + k + 1)
                    nc.scalar.activation(dst, SETS[which][0:DA, 0:NP], ACT.Copy).then_inc(s_projc, 1)
                if n == 0:
                    act.wait_ge(s_zeroed, 16)
                for i in range(T):
                    act.wait_ge(s_neg[n], i + 1)
                    nc.scalar.activation(probs[:, i, :], SETS[i % 2][:, 0:N], ACT.Exp, bias=negmax[:, i:i + 1],
                                         accum_out=zsum[:, i:i + 1])
                    nc.scalar.activation(cand[:, i, 0:8 * CHUNKS[n]], cand[:, i, 0:8 * CHUNKS[n]], ACT.Exp, bias=negmax[:, i:i + 1]).then_inc(s_exp[n], 1)
                rdst = f1 if n == 0 else xraw
                for i in range(T):
                    act.wait_ge(s_r[n], i + 1)
                    if n == 0:
                        nc.scalar.activation(rrow[:, i:i + 1], psum[:, 6 + i % 2, D:D + 1], ACT.Copy)
                    nc.scalar.activation(rdst[:, i, 0:D], psum[:, 6 + i % 2, 0:D], ACT.Copy).then_inc(s_rc[n], 1)
                adst = a1 if n == 0 else f1
                for i in range(T + 1):
                    if i < T:
                        act.wait_ge(s_pt[n], i + 1)
                        if i >= 2:
                            act.wait_ge(s_a[n], i - 1)
                        pt = p_t[:, i % 2, :, :].rearrange("p t n -> p (t n)")
                        nc.scalar.activation(pt[:, 0:NP - P], SETS[i % 2][:, 0:NP - P], ACT.Copy)
                        nc.scalar.activation(pt[0:LAST, NP - P:NP], SETS[i % 2][0:LAST, NP - P:NP], ACT.Copy).then_inc(s_ptc[n], 1)
                    if i >= 1:
                        j = i - 1
                        act.wait_ge(s_a[n], j + 1)
                        nc.scalar.activation(adst[:, j, 0:D], psum[:, 6 + j % 2, 0:D], ACT.Copy, scale=rkept[:, j:j + 1]).then_inc(s_ac[n], 1)
                if n == 0:
                    copy_out(t_f1, 0, 2)
                    copy_out(t_a, 1, 3)
                else:
                    copy_out(t_a2, 1, 4)
                    copy_out(t_f2, 0, 5)
            for i in range(T):
                act.wait_ge(s_h, i + 1)
                nc.scalar.activation(hrow[:, i, :], psum[:, 6 + i % 2, 0:D], ACT.Copy).then_inc(s_hc, 1)
            std(2)
            std(3)
            copy_out(t_a, 0, 6)
            act.wait_ge(s_gd, 1)
            nc.scalar.activation(gexp, gdiff, ACT.Exp).then_inc(s_ge, 1)
            act.wait_ge(s_cbt, 1)
            nc.scalar.activation(comb_t[:, :], SETS[1][0:E, 0:NP], ACT.Copy).then_inc(s_cbtc, 1)
            nc.scalar.drain().then_inc(s_hf, 2)
            nc.scalar.drain().then_inc(s_ys, 16)

            def body(r):
                def group(g):
                    for s in range(SLOTS):
                        e = g * SLOTS + s
                        act.wait_ge(s_hp, r * E + e + 1)
                        if s >= 2:
                            act.wait_ge(s_y, SLOTS + r * E + e - 1)
                        for c in range(FC):
                            last = nc.scalar.activation(hid[:, s % 2, c, 0:CAP], psum[:, 2 + s % 2, c * CAP:(c + 1) * CAP], ACT.Relu,
                                                        bias=eb1s[:, bass.ds(e * FC + c, 1)])
                        last.then_inc(s_hf, 1)
                    act.wait_ge(s_yf, r * E + g * SLOTS + SLOTS + 2)
                    act.dma_start(slot_y[bass.ds(g * (SLOTS * CAP), SLOTS * CAP), :].rearrange("(e c) d -> c e d", c=CAP), ysb[0:CAP, :, :]).then_inc(s_ys, 16)
                with act.Fori(0, GROUPS) as g:
                    group(g)
            each_round(act, body)

        @block.vector
        def _(dve):
            V = nc.vector

            def settle():
                V.drain()

            def variance(src, k):
                for i in range(T):
                    V.bn_stats(stats[:, i, :], src(i))
                settle()
                for i in range(T):
                    V.bn_aggr(mv[:, i, :], stats[:, i, :])
                settle()
                V.tensor_scalar(rstd[:, :], mv[:, :, 1], EPS, None, ALU.add).then_inc(s_var, 1)
                dve.wait_ge(s_std, k)
                V.reciprocal(rstd[:, :], rstd[:, :])
                settle()

            def normalise(src, dst, k):
                variance(src, k)
                for i in range(T):
                    V.tensor_scalar(dst(i), src(i), mv[:, i, 0:1], rstd[:, i:i + 1], ALU.subtract, ALU.mult)
                settle()

            V.memset(f0[:, :, D:D + 1], 1.0)
            dve.wait_ge(s_x, 16)
            normalise(lambda i: xraw[:, i, :], lambda i: f0[:, i, 0:D], 1)
            V.memset(f1[:, :, D:D + 1], 1.0)
            V.drain().then_inc(s_norm, 1)

            def cumulate(a, b, eight):
                for j in range(8):
                    V.tensor_tensor(cum[:, a:b, j + 1], cum[:, a:b, j], eight[:, :, j], ALU.add)
                    settle()

            def update(a, b):
                V.tensor_tensor(yes[:, a:b], mass[:, a:b], target[:, a:b], ALU.is_lt)
                V.tensor_tensor(no[:, a:b], mass[:, a:b], target[:, a:b], ALU.is_ge)
                settle()
                V.copy_predicated(hi[:, a:b], yes[:, a:b], mid[:, a:b])
                V.copy_predicated(above[:, a:b], yes[:, a:b], mass[:, a:b])
                V.copy_predicated(lo[:, a:b], no[:, a:b], mid[:, a:b])
                settle()

            def row_mass(i):
                V.scalar_tensor_tensor(out=below[:, :], in0=probs[:, i, :], scalar=mid[:, i:i + 1], in1=probs[:, i, :],
                                       op0=ALU.is_ge, op1=ALU.mult, accum_out=mass[:, i:i + 1])
                settle()

            def halve_row(i):
                lo_i, hi_i, mid_i = (a[:, i:i + 1].bitcast(I32) for a in (lo, hi, mid))
                V.tensor_tensor(low_i[:, i:i + 1], lo_i, hi_i, ALU.bitwise_xor)
                V.tensor_tensor(high_i[:, i:i + 1], lo_i, hi_i, ALU.bitwise_and)
                settle()
                V.tensor_scalar(low_i[:, i:i + 1], low_i[:, i:i + 1], 1, None, ALU.arith_shift_right)
                settle()
                V.tensor_tensor(mid_i, low_i[:, i:i + 1], high_i[:, i:i + 1], ALU.add)
                settle()
                row_mass(i)
                update(i, i + 1)

            def read_cut(a, b, to, eight, d, w):
                V.tensor_copy(cum[:, a:b, 0], above[:, a:b])
                settle()
                cumulate(a, b, eight)
                V.tensor_tensor(d, cum[:, a:b, 0:8], target[:, a:b].unsqueeze(2).broadcast_to([P, b - a, 8]), ALU.is_ge)
                settle()
                V.scalar_tensor_tensor(out=w, in0=d, scalar=4.0, in1=eight, op0=ALU.mult, op1=ALU.add)
                settle()
                V.tensor_reduce(to[:, a:b], w, axis=AX.X, op=ALU.min)
                settle()
                V.tensor_tensor(w, d, eight, ALU.mult)
                settle()
                V.tensor_reduce(mass[:, a:b], w, axis=AX.X, op=ALU.max)
                settle()
                V.tensor_tensor(mass[:, a:b], mass[:, a:b], to[:, a:b], ALU.is_ge)
                V.tensor_scalar(flags[:, a:b], d[:, :, 7], -1.0, 1.0, ALU.mult, ALU.add)
                settle()

            def any_flag(flags, a, b):
                V.tensor_reduce(flag32[:, 0:1], flags[:, a:b], axis=AX.X, op=ALU.max)
                settle()
                V.transpose(flag32t[:, :], flag32[:, :])
                settle()
                V.tensor_reduce(flag1[:, :], flag32t[:, :], axis=AX.X, op=ALU.max)
                settle()
                V.tensor_copy(flag_i[:, :], flag1[:, :])
                settle()
                four = [dve.value_load(flag_i[q:q + 1, 0:1], min_val=0, max_val=2) for q in range(0, P, 32)]
                return four[0] + four[1] + four[2] + four[3]

            def exact_row(i, scan):
                one = slice(i, i + 1)
                V.tensor_scalar(lo[:, one], zsum[:, one], (1.0 - TOP_P) / (2 * N), None, ALU.mult)
                V.memset(hi[:, one], 2.0)
                V.memset(above[:, one], 0.0)
                settle()
                with dve.Fori(0, EXACT):
                    halve_row(i)
                V.tensor_copy(cut[:, one], lo[:, one])
                V.tensor_tensor(mass[:, one], target[:, one], above[:, one], ALU.subtract)
                V.reciprocal(kept[:, one], lo[:, one])
                settle()
                V.tensor_tensor(mass[:, one], mass[:, one], kept[:, one], ALU.mult)
                settle()
                V.tensor_scalar(mass[:, one], mass[:, one], 1.0, None, ALU.add)
                V.tensor_scalar(below[:, :], probs[:, i, :], cut[:, one], None, ALU.is_equal)
                settle()
                V.tensor_tensor_scan(scan, below[:, :], below[:, :], 0.0, ALU.add, ALU.max)
                settle()
                V.tensor_tensor(below[:, :], below[:, :], scan, ALU.mult)
                settle()
                V.scalar_tensor_tensor(out=probs[:, i, :], in0=below[:, :], scalar=mass[:, one], in1=probs[:, i, :],
                                       op0=ALU.is_lt, op1=ALU.mult)
                V.memset(ties[:, one], 0.0)
                settle()

            def retry_row(i, scan):
                one = slice(i, i + 1)
                V.tensor_copy(opened[:, :], flags[:, one])
                V.tensor_tensor(yes[:, one], hidden[:, one], cut[:, one], ALU.is_ge)
                V.memset(redone[:, 0, 0:1], 2.0)
                V.memset(redone[:, 0, 1:2], 0.0)
                V.tensor_scalar(mid[:, one], hidden[:, one], 1.0 + 2.0 ** -20, None, ALU.mult)
                settle()
                V.copy_predicated(hi[:, one], yes[:, one], redone[:, 0, 0:1])
                V.copy_predicated(above[:, one], yes[:, one], redone[:, 0, 1:2])
                V.tensor_tensor(mid[:, one], mid[:, one], lo[:, one], ALU.max)
                settle()
                row_mass(i)
                update(i, i + 1)
                with dve.Fori(0, RETRY):
                    halve_row(i)
                V.scalar_tensor_tensor(out=below[:, :], in0=probs[:, i, :], scalar=hi[:, one], in1=probs[:, i, :],
                                       op0=ALU.is_lt, op1=ALU.mult)
                settle()
                V.max(retop[:, 0, :], below[:, :])
                settle()
                read_cut(i, i + 1, found, retop[:, :, :], redone[:, :, :], work8[:, i:i + 1, :])
                V.copy_predicated(cut[:, one], opened[:, :], found[:, one])
                V.copy_predicated(ties[:, one], opened[:, :], mass[:, one])
                V.copy_predicated(etop[:, i, :], opened[:, :].broadcast_to([P, 8]), retop[:, 0, :])
                V.copy_predicated(done8[:, i, :], opened[:, :].broadcast_to([P, 8]), redone[:, 0, :])
                V.tensor_tensor(flags[:, one], flags[:, one], opened[:, :], ALU.mult)
                settle()
                with dve.If(any_flag(flags, i, i + 1) > 0):
                    exact_row(i, scan)

            V.memset(flag32[:, :], 0.0)
            V.memset(one_i[:, :], 1)
            dve.wait_ge(s_col, 1)
            for n in range(STEPS):
                width, chunk_count = WIDTH[n], CHUNKS[n]
                cands = 8 * chunk_count
                for i in range(T):
                    dve.wait_ge(s_lg[n], i + 1)
                    for c in range(chunk_count):
                        V.max(cand[:, i, 8 * c:8 * c + 8], SETS[i % 2][:, c * width:min(N, (c + 1) * width)])
                    settle()
                    V.tensor_reduce(negmax[:, i:i + 1], cand[:, i, 0:cands:8], axis=AX.X, op=ALU.max)
                    settle()
                    V.tensor_scalar(negmax[:, i:i + 1], negmax[:, i:i + 1], -1.0, None, ALU.mult).then_inc(s_neg[n], 1)
                for a, b in PARTS:
                    dve.wait_ge(s_exp[n], b)
                    V.tensor_scalar(target[:, a:b], zsum[:, a:b], TOP_P, None, ALU.mult)
                    V.tensor_scalar(lo[:, a:b], zsum[:, a:b], (1.0 - TOP_P) / (2 * N), None, ALU.mult)
                    V.memset(hi[:, a:b], 2.0)
                    V.memset(above[:, a:b], 0.0)
                    V.tensor_reduce(hidden[:, a:b], cand[:, a:b, 7:cands:8], axis=AX.X, op=ALU.max)
                    settle()
                    for k in range(STEPS_OF_CUT[n]):
                        V.tensor_scalar(mid[:, a:b], lo[:, a:b], 2.0 ** (RANGE / 2 ** (k + 1)), None, ALU.mult)
                        settle()
                        for i in range(a, b):
                            V.scalar_tensor_tensor(out=junk[:, i - a, 0:cands], in0=cand[:, i, 0:cands], scalar=mid[:, i:i + 1], in1=cand[:, i, 0:cands],
                                                   op0=ALU.is_ge, op1=ALU.mult, accum_out=mass[:, i:i + 1])
                        settle()
                        update(a, b)
                    for i in range(a, b):
                        V.scalar_tensor_tensor(out=picked[:, i % 2, 0:cands], in0=cand[:, i, 0:cands], scalar=hi[:, i:i + 1], in1=cand[:, i, 0:cands],
                                               op0=ALU.is_lt, op1=ALU.mult)
                        settle()
                        V.max(etop[:, i, :], picked[:, i % 2, 0:cands])
                    settle()
                    read_cut(a, b, cut, etop[:, a:b, :], done8[:, a:b, :], work8[:, a:b, :])
                    V.tensor_copy(ties[:, a:b], mass[:, a:b])
                    settle()
                    V.tensor_tensor(mass[:, a:b], hidden[:, a:b], cut[:, a:b], ALU.is_ge)
                    settle()
                    V.tensor_tensor(flags[:, a:b], flags[:, a:b], mass[:, a:b], ALU.max)
                    settle()
                    scan = cand[:, a:b, :].rearrange("p t c -> p (t c)")[:, 0:N]
                    with dve.If(any_flag(flags, a, b) > 0):
                        for i in range(a, b):
                            with dve.If(any_flag(flags, i, i + 1) > 0):
                                retry_row(i, scan)
                    def finish(i):
                        settle()
                        V.scalar_tensor_tensor(out=kept[:, i:i + 1], in0=zsum[:, i:i + 1], scalar=1e-12, in1=kept[:, i:i + 1], op0=ALU.mult, op1=ALU.max)
                        settle()
                        V.reciprocal(rkept[:, i:i + 1], kept[:, i:i + 1]).then_inc(s_mask[n], 1)

                    with dve.If(any_flag(ties, a, b) > 0):
                        V.tensor_tensor(high_i[:, a:b], cut[:, a:b].bitcast(I32), one_i[:, a:b], ALU.add)
                        V.tensor_tensor(last7[:, a:b, :], done8[:, a:b, 1:8], done8[:, a:b, 0:7], ALU.subtract)
                        settle()
                        V.tensor_tensor(lo[:, a:b], high_i[:, a:b].bitcast(F32), cut[:, a:b], ALU.subtract)
                        settle()
                        V.tensor_tensor(lo[:, a:b], lo[:, a:b], ties[:, a:b], ALU.mult)
                        for i in range(a, b):
                            V.max_index(place[:, i, :], etop[:, i, :], probs[:, i, :])
                        settle()
                        V.tensor_copy(work8[:, a:b, :], place[:, a:b, :])
                        settle()
                        V.tensor_tensor(work8[:, a:b, 0:7], work8[:, a:b, 0:7], last7[:, a:b, :], ALU.mult)
                        settle()
                        V.tensor_reduce(mid[:, a:b], work8[:, a:b, 0:7], axis=AX.X, op=ALU.add)
                        settle()
                        for i in range(a, b):
                            V.tensor_scalar(raised, column, mid[:, i:i + 1], lo[:, i:i + 1], ALU.is_gt, ALU.mult)
                            settle()
                            V.scalar_tensor_tensor(out=below[:, :], in0=raised, scalar=cut[:, i:i + 1], in1=probs[:, i, :],
                                                   op0=ALU.add, op1=ALU.is_le)
                            settle()
                            V.scalar_tensor_tensor(out=probs[:, i, :], in0=below[:, :], scalar=1.0, in1=probs[:, i, :],
                                                   op0=ALU.mult, op1=ALU.mult, accum_out=kept[:, i:i + 1])
                            finish(i)
                    with dve.Else():
                        for i in range(a, b):
                            V.scalar_tensor_tensor(out=probs[:, i, :], in0=probs[:, i, :], scalar=cut[:, i:i + 1], in1=probs[:, i, :],
                                                   op0=ALU.is_ge, op1=ALU.mult, accum_out=kept[:, i:i + 1])
                            finish(i)
                dve.wait_ge(s_rc[n], T)
                if n == 0:
                    V.reciprocal(rinv[:, :], rrow[:, :])
                    settle()
                rdst = f1[:, :, 0:D] if n == 0 else xraw[:, :, :]
                V.tensor_tensor(rdst, rdst, rinv[:, :].unsqueeze(2).broadcast_to([P, T, D]), ALU.mult).then_inc(s_rs[n], 1)

            dve.wait_ge(s_hc, T)
            dve.wait_ge(s_xr, 16 * 5)
            dve.wait_ge(s_te, 5)
            dve.wait_ge(s_h, T)
            variance(lambda i: hrow[:, i, :], 2)
            for i in range(T):
                V.tensor_scalar(tmp[:, i, :], hrow[:, i, :], mv[:, i, 0:1], rstd[:, i:i + 1], ALU.subtract, ALU.mult)
            settle()
            V.tensor_tensor(tmp, tmp, gs[:, :].unsqueeze(1).broadcast_to([P, T, D]), ALU.mult)
            settle()
            V.tensor_tensor(tmp, tmp, bs[:, :].unsqueeze(1).broadcast_to([P, T, D]), ALU.add)
            settle()
            V.tensor_tensor(x1, tmp, xraw[:, :, :], ALU.add)
            settle()
            normalise(lambda i: x1[:, i, :], lambda i: xn[:, i, :], 3)
            V.drain().then_inc(s_norm, 1)
            dve.wait_ge(s_rl, 1)
            V.tensor_tensor(lg, SETS[1][:, 0:T * E].rearrange("p (t e) -> p t e", t=T), brs[:, :].unsqueeze(1).broadcast_to([P, T, E]), ALU.add).then_inc(s_rlc, 1)
            settle()
            for i in range(T):
                V.max(top[:, i, :], lg[:, i, :])
            settle()
            for i in range(T):
                V.max_index(idx8[:, i, :], top[:, i, :], lg[:, i, :])
            V.tensor_tensor(gdiff, top[:, :, 1], top[:, :, 0], ALU.subtract).then_inc(s_gd, 1)
            settle()
            for k in range(2):
                V.tensor_copy(eidx[:, k, :], idx8[:, :, k])
            settle()
            for k, m in enumerate((m1, m2)):
                V.tensor_tensor(m, iota.unsqueeze(1).broadcast_to([P, T, E]), eidx[:, k, :].unsqueeze(2).broadcast_to([P, T, E]), ALU.is_equal)
            settle()
            for m in (m1, m2):
                V.tensor_scalar(m[:, T - 1, :], m[:, T - 1, :], real, None, ALU.mult)
            settle()
            V.tensor_tensor(mm, m1, m2, ALU.add)
            settle()
            V.tensor_copy(macc[:, 0, :], mm[:, 0, :])
            settle()
            for i in range(1, T):
                V.tensor_tensor(macc[:, i, :], macc[:, i - 1, :], mm[:, i, :], ALU.add)
                settle()
            V.drain().then_inc(s_m, 1)
            dve.wait_ge(s_ge, 1)
            V.tensor_scalar(gdiff, gexp, 1.0, None, ALU.add)
            settle()
            V.reciprocal(gate[:, 0, :], gdiff)
            settle()
            V.tensor_tensor(gate[:, 1, :], gexp, gate[:, 0, :], ALU.mult)
            settle()
            V.tensor_tensor(comb, m1, gate[:, 0, :].unsqueeze(2).broadcast_to([P, T, E]), ALU.mult)
            V.tensor_tensor(prod, m2, gate[:, 1, :].unsqueeze(2).broadcast_to([P, T, E]), ALU.mult)
            settle()
            V.tensor_tensor(comb, comb, prod, ALU.add)
            V.drain().then_inc(s_cb, 1)
            dve.wait_ge(s_rk, 1)
            V.tensor_copy(ranks, SETS[0][:, 0:T * E].rearrange("p (t e) -> p t e", t=T))
            V.tensor_reduce(most, SETS[0][:, T * E:(T + 1) * E], axis=AX.X, op=ALU.max)
            settle()
            V.tensor_copy(most_i, most)
            V.drain().then_inc(s_rkc, 1)
            V.drain().then_inc(s_most, 1)
            for k, m in enumerate((m1, m2)):
                V.tensor_tensor(prod, ranks, m, ALU.mult)
                settle()
                V.tensor_reduce(rank[:, k, :], prod, axis=AX.X, op=ALU.add)
                settle()
            V.tensor_scalar(flag1[:, :], real, -FAR, FAR, ALU.mult, ALU.add)
            settle()
            for k in range(2):
                V.tensor_scalar(rank[:, k, T - 1:T], rank[:, k, T - 1:T], flag1[:, 0:1], None, ALU.add)
            V.tensor_scalar(base[:, :, :], eidx[:, :, :], float(CAP), -FAR, ALU.mult, ALU.add)
            settle()
            dve.wait_ge(s_b2, 1)
            V.tensor_tensor(acc[:, :, :], SETS[0][:, 0:NP].rearrange("p (t d) -> p t d", t=T), x1, ALU.add)
            settle()
            V.drain().then_inc(s_xtf, 2)
            V.drain().then_inc(s_yf, 2)

            def body(r):
                V.tensor_scalar(ok1[:, :, :], rank[:, :, :], 0.0, None, ALU.is_ge)
                V.tensor_scalar(ok2[:, :, :], rank[:, :, :], float(CAP), None, ALU.is_lt)
                V.tensor_tensor(slot[:, :, :], base[:, :, :], rank[:, :, :], ALU.add)
                settle()
                V.tensor_tensor(ok1[:, :, :], ok1[:, :, :], ok2[:, :, :], ALU.mult)
                settle()
                V.tensor_tensor(slot[:, :, :], slot[:, :, :], ok1[:, :, :], ALU.mult)
                settle()
                V.tensor_scalar(slot_i[:, :, :], slot[:, :, :], FAR, None, ALU.add)
                V.tensor_scalar(rank[:, :, :], rank[:, :, :], float(-CAP), None, ALU.add)
                V.memset(yg, 0.0)
                V.drain().then_inc(s_slot, 1)
                for b in range(E // 4):
                    dve.wait_ge(s_xt, r * (E // 4) + b + 1)
                    V.tensor_copy(xgt[:, 4 * b:4 * b + 4, :], psum[:, b % 2, 0:4 * CAP].rearrange("p (e c) -> p e c", e=4)).then_inc(s_xtf, 1)

                def group(g):
                    dve.wait_ge(s_ys, r * (GROUPS * 16) + g * 16 + 16)
                    for s in range(SLOTS):
                        e = g * SLOTS + s
                        dve.wait_ge(s_y, SLOTS + r * E + e + 1)
                        V.tensor_copy(ysb[0:CAP, s, :], psum[0:CAP, 4 + s % 2, 0:D]).then_inc(s_yf, 1)
                with dve.Fori(0, GROUPS) as g:
                    group(g)
                dve.wait_ge(s_yg, (r + 1) * (2 * T * 16))
                for k in range(2):
                    V.tensor_tensor(yg[:, k, :, :], yg[:, k, :, :], gate[:, k, :].unsqueeze(2).broadcast_to([P, T, D]), ALU.mult)
                    settle()
                    V.tensor_tensor(acc[:, :, :], acc[:, :, :], yg[:, k, :, :], ALU.add)
                    settle()
            each_round(dve, body)
            V.drain().then_inc(s_acc, 1)


def kernel(x, adj, L0_gnn_W1, L0_gnn_W2, L0_gnn_W3, L0_gnn_U1, L0_gnn_U2, L0_gnn_ln_g, L0_gnn_ln_b,
           L0_ffn_Wr, L0_ffn_br, L0_ffn_W1, L0_ffn_b1, L0_ffn_W2, L0_ffn_b2):
    import numpy as np
    import concourse.bacc as bacc
    from concourse.bass_utils import run_bass_kernel_spmd

    f = np.float32
    pad = NP - N
    consts = np.concatenate([np.eye(P, dtype=f), np.triu(np.ones((P, P), f), 1), np.ones((P, P), f),
                             np.broadcast_to(np.arange(E, dtype=f), (P, E)),
                             (np.arange(P) < LAST).astype(f)[:, None]], axis=1)
    adj = np.asarray(adj)
    x = np.asarray(x)
    arrays = {
        "x": np.concatenate([x, x[:pad]], axis=0),
        "adj_t": np.concatenate([adj.T, adj.T[:, :pad]], axis=1),
        "w1_t": np.asarray(L0_gnn_W1).T,
        "w2_t": np.asarray(L0_gnn_W2).T,
        "w3_t": np.asarray(L0_gnn_W3).T,
        "u_t": np.concatenate([np.asarray(u)[n].T for u in (L0_gnn_U1, L0_gnn_U2) for n in range(STEPS)], axis=0),
        "ln_g": np.broadcast_to(np.asarray(L0_gnn_ln_g), (P, D)),
        "ln_b": np.broadcast_to(np.asarray(L0_gnn_ln_b), (P, D)),
        "wr": np.asarray(L0_ffn_Wr),
        "br": np.broadcast_to(np.asarray(L0_ffn_br), (P, E)),
        "ew1": np.asarray(L0_ffn_W1).reshape(E * D, F),
        "eb1": np.asarray(L0_ffn_b1).reshape(E * FC, P).T,
        "ew2": np.asarray(L0_ffn_W2).reshape(E * F, D),
        "eb2": np.asarray(L0_ffn_b2),
        "consts": consts,
    }
    nc = bacc.Bacc("TRN2", target_bir_lowering=False, num_devices=1)
    arrays = {f"in_{k}": np.ascontiguousarray(v) for k, v in arrays.items()}
    args = [nc.dram_tensor(k, v.shape, mybir.dt.from_np(v.dtype), kind="ExternalInput").ap() for k, v in arrays.items()]
    out = nc.dram_tensor("out_0", (N, D), mybir.dt.float32, kind="ExternalOutput").ap()
    build(nc, *args, out)
    return run_bass_kernel_spmd(nc, [arrays], core_ids=[0]).results[0]["out_0"]
```

```python
import math
from contextlib import ExitStack

import concourse.bass as bass
from concourse import mybir

P = 128
N = 1354
D = 128
DA = 64
STEPS = 2
TOP_P = 0.9
EPS = 1e-5
T = -(-N // P)
NP = T * P
LAST = N - (T - 1) * P
E = 64
F = 256
FC = F // P
CAP = 96
ROUNDS = -(-N // CAP)
SLOTS = 16
GROUPS = E // SLOTS
HALF = SLOTS // 2
WIDTH = (113, 25)
CHUNKS = tuple(N // w for w in WIDTH)
RANGE = math.log2(2 * N / (1.0 - TOP_P)) + 0.1
STEPS_OF_CUT = (6, 10)
RETRY = 6
PARTS = ((0, 6), (6, T))
EXACT = 32
BANK = 512
BANK_TILES = [(t, min(t + BANK // P, T)) for t in range(0, T, BANK // P)]
FAR = float(E * CAP * 2)


def build(nc, x, adj_t, w1_t, w2_t, w3_t, u_t, ln_g, ln_b, wr, br, ew1, eb1, ew2, eb2, consts, out):
    BF16 = mybir.dt.bfloat16
    F32, I32, U32 = mybir.dt.float32, mybir.dt.int32, mybir.dt.uint32
    ALU = mybir.AluOpType
    ACT = mybir.ActivationFunctionType
    AX = mybir.AxisListType

    slot_x = nc.dram_tensor("slot_x", [E * CAP, D], F32, kind="Internal").ap()
    slot_y = nc.dram_tensor("slot_y", [E * CAP, D], F32, kind="Internal").ap()

    with ExitStack() as ctx:
        def sb(name, shape, dt=F32):
            return ctx.enter_context(nc.sbuf_tensor(name, shape, dt))

        def sem(name):
            return ctx.enter_context(nc.semaphore(name))

        adj = sb("adj", [P, T, NP])
        probs = sb("probs", [P, T, N])
        xraw = sb("xraw", [P, T, D])
        f0 = sb("f0", [P, T, D + 1])
        f1 = sb("f1", [P, T, D + 1])
        a1 = sb("a1", [P, T, D])
        t_a = sb("t_a", [P, NP])
        t_a2 = sb("t_a2", [P, NP])
        t_f1 = sb("t_f1", [P, NP])
        t_f2 = sb("t_f2", [P, NP])
        p_t = sb("p_t", [P, 2, T, P])
        q_t, k_t = (p_t[0:DA, b, :, :].rearrange("p t n -> p (t n)") for b in range(2))
        below = t_a2[:, 0:N]
        cand = sb("cand", [P, T, 8 * max(CHUNKS)])
        picked = below[:, 0:2 * 8 * max(CHUNKS)].rearrange("p (b c) -> p b c", b=2)
        column = t_f2[:, 0:N // 2].bitcast(mybir.dt.int16)
        raised = t_f2[:, N // 2:N].bitcast(BF16)
        most_tiles = max(b - a for a, b in PARTS)
        junk = t_a2[:, :].bitcast(BF16)[:, 0:most_tiles * 8 * max(CHUNKS)].rearrange("p (t c) -> p t c", t=most_tiles)
        w1s = sb("w1s", [D, DA])
        w2s = sb("w2s", [DA, DA])
        w3s = sb("w3s", [D, DA])
        us = sb("us", [P, 2 * STEPS, D])
        wrs = sb("wrs", [D, E])
        brs = sb("brs", [P, E])
        cs = sb("cs", [P, 3 * P + E + 1])
        ident, tri, ones = cs[:, 0:P], cs[:, P:2 * P], cs[:, 2 * P:3 * P]
        iota = cs[:, 3 * P:3 * P + E]
        real = cs[:, 3 * P + E:3 * P + E + 1]
        stats = sb("stats", [P, T, 6])
        mv = sb("mv", [P, T, 2])
        rstd = sb("rstd", [P, T])
        etop = sb("etop", [P, T, 8])
        negmax = sb("negmax", [P, T])
        cum = sb("cum", [P, T, 9])
        done8 = sb("done8", [P, T, 8])
        work8 = sb("work8", [P, T, 8])
        zsum = sb("zsum", [P, T])
        target = sb("target", [P, T])
        lo = sb("lo", [P, T])
        hi = sb("hi", [P, T])
        mid = sb("mid", [P, T])
        mass = sb("mass", [P, T])
        above = sb("above", [P, T])
        found = sb("found", [P, T])
        hidden = sb("hidden", [P, T])
        one_i = sb("one_i", [P, T], I32)
        last7 = sb("last7", [P, T, 7])
        place = sb("place", [P, T, 8], U32)
        retop = sb("retop", [P, 1, 8])
        redone = sb("redone", [P, 1, 8])
        both = sb("both", [P, 2, T])
        both_i = sb("both_i", [1, 2, T], I32)
        some_i = sb("some_i", [1, 2], I32)
        some = sb("some", [1, 2])
        flags, ties = both[:, 0, :], both[:, 1, :]
        opened = sb("opened", [P, 1], U32)
        flag32 = sb("flag32", [P, 32])
        flag32t = sb("flag32t", [P, 32])
        low_i = sb("low_i", [P, T], I32)
        high_i = sb("high_i", [P, T], I32)
        yes = sb("yes", [P, T], U32)
        no = sb("no", [P, T], U32)
        cut = sb("cut", [P, T])
        flag1 = sb("flag1", [P, 1])
        flag_i = sb("flag_i", [P, 1], I32)
        kept = sb("kept", [P, T])
        rkept = sb("rkept", [P, T])
        rrow = sb("rrow", [P, T])
        rinv = sb("rinv", [P, T])

        flat_p = probs[:, :, :].rearrange("p t n -> p (t n)")
        xg = flat_p[0:CAP, 0:E * D].rearrange("p (e d) -> p e d", e=E)
        xgt = flat_p[:, E * D:E * D + E * CAP].rearrange("p (e c) -> p e c", e=E)
        late = flat_p[:, E * D + E * CAP:E * D + E * CAP + 4 * D].rearrange("p (k d) -> p k d", k=4)
        gs, bs, eb1s, eb2s = late[:, 0, :], late[:, 1, :], late[:, 2, :], late[0:E, 3, :]
        zero = flat_p[:, 0:E * CAP * D // P]
        flat_s = adj[:, :, :].rearrange("p t n -> p (t n)")
        at = 0

        def region(n):
            nonlocal at
            at += n
            return flat_s[:, at - n:at]

        rw1 = region(SLOTS * F).rearrange("p (s f) -> p s f", s=SLOTS)
        rw2 = region(SLOTS * FC * D).rearrange("p (s c d) -> p s c d", s=SLOTS, c=FC)
        ysb = region(SLOTS * D).rearrange("p (s d) -> p s d", s=SLOTS)
        yg = region(2 * T * D).rearrange("p (k t d) -> p k t d", k=2, t=T)
        hid = region(2 * FC * P).rearrange("p (b c n) -> p b c n", b=2, c=FC)
        assert at <= T * NP
        flat_pt = p_t[:, :, :, :].rearrange("p b t n -> p (b t n)")
        lg = flat_pt[:, 0:T * E].rearrange("p (t e) -> p t e", t=T)
        m1 = flat_pt[:, T * E:2 * T * E].rearrange("p (t e) -> p t e", t=T)
        m2 = flat_pt[:, 2 * T * E:3 * T * E].rearrange("p (t e) -> p t e", t=T)
        flat_f1 = f1[:, :, :].rearrange("p t n -> p (t n)")
        mm = flat_f1[:, 0:T * E].rearrange("p (t e) -> p t e", t=T)
        macc = t_a2[:, 0:(T + 1) * E].rearrange("p (t e) -> p t e", t=T + 1)
        comb = flat_pt[:, 3 * T * E:4 * T * E].rearrange("p (t e) -> p t e", t=T)
        comb_t = t_a[0:E, :]
        ranks = t_f1[:, 0:T * E].rearrange("p (t e) -> p t e", t=T)
        prod = t_f1[:, T * E:2 * T * E].rearrange("p (t e) -> p t e", t=T)
        hrow = a1
        xn = xraw_n = f0[:, :, 0:D]
        x1 = t_f2[:, :].rearrange("p (t d) -> p t d", t=T)
        tmp = t_a2[:, :].rearrange("p (t d) -> p t d", t=T)
        acc = a1
        flat_c = cand[:, :, :].rearrange("p t c -> p (t c)")
        used = 0

        def small(*shape, dt=F32):
            nonlocal used
            size = math.prod(shape)
            used += size
            piece = flat_c[:, used - size:used]
            piece = piece if dt is F32 else piece.bitcast(dt)
            return piece if len(shape) == 1 else piece.rearrange("p (a b) -> p a b", a=shape[0])

        top = small(T, 8)
        idx8 = small(T, 8, dt=U32)
        eidx = small(2, T)
        rank = small(2, T)
        base = small(2, T)
        ok1 = small(2, T)
        ok2 = small(2, T)
        slot = small(2, T)
        slot_i = small(2, T, dt=I32)
        gate = small(2, T)
        gdiff = small(T)
        gexp = small(T)
        most = small(1)
        most_i = small(1, dt=I32)

        psum = ctx.enter_context(nc.psum_tensor("psum", [P, 8, 512], F32))
        flat = psum[:, :, :].rearrange("p b n -> p (b n)")
        SETS = [flat[:, 0:1536], flat[:, 1536:3072]]
        counts = SETS[1][0:1, NP:NP + 2 * T].rearrange("p (k t) -> p k t", k=2)

        s_x, s_adj, s_w, s_xr = sem("x_loaded"), sem("adj_loaded"), sem("weights_loaded"), sem("x_reloaded")
        s_zero, s_zeroed = sem("zero_tile_ready"), sem("slots_zeroed")
        s_col = sem("column_numbers_ready")
        s_flag, s_flagsum = sem("flags_ready"), sem("flags_summed")
        s_var, s_std = sem("variance_ready"), sem("std_ready")
        s_norm = sem("rows_normalised")
        s_tp, s_te = sem("transposes_done"), sem("transposes_copied")
        s_proj, s_projc = sem("projections_done"), sem("projections_copied")
        s_lg = [sem(f"logits_ready{n}") for n in range(STEPS)]
        s_neg = [sem(f"negmax_ready{n}") for n in range(STEPS)]
        s_exp = [sem(f"exp_done{n}") for n in range(STEPS)]
        s_r = [sem(f"adj_product_ready{n}") for n in range(STEPS)]
        s_rc = [sem(f"adj_product_copied{n}") for n in range(STEPS)]
        s_rs = [sem(f"adj_product_scaled{n}") for n in range(STEPS)]
        s_mask = [sem(f"kept_ready{n}") for n in range(STEPS)]
        s_scale = [sem(f"kept_scale_ready{n}") for n in range(STEPS)]
        s_pt = [sem(f"kept_transposed{n}") for n in range(STEPS)]
        s_ptc = [sem(f"kept_transpose_copied{n}") for n in range(STEPS)]
        s_a = [sem(f"attention_ready{n}") for n in range(STEPS)]
        s_ac = [sem(f"attention_copied{n}") for n in range(STEPS)]
        s_h, s_hc = sem("h_ready"), sem("h_copied")
        s_rl, s_rlc = sem("router_logits_ready"), sem("router_logits_read")
        s_gd, s_ge = sem("gate_difference_ready"), sem("gate_exp_ready")
        s_m, s_rk, s_rkc = sem("choices_ready"), sem("ranks_ready"), sem("ranks_read")
        s_cb, s_cbt, s_cbtc, s_b2 = sem("combine_ready"), sem("combine_transposed"), sem("combine_copied"), sem("bias_ready")
        s_most = sem("largest_count_ready")
        s_slot, s_sent = sem("slots_ready"), sem("tokens_sent")
        s_xg = [sem(f"tokens_loaded_{q}") for q in range(GROUPS)]
        s_wl = [sem(f"expert_weights{s}") for s in range(SLOTS)]
        s_pass = sem("wait_passed")
        s_xt, s_xtf = sem("tokens_transposed"), sem("transpose_banks_freed")
        s_hp, s_hf = sem("hidden_ready"), sem("hidden_banks_freed")
        s_y, s_yf = sem("expert_out_ready"), sem("out_banks_freed")
        s_ys = sem("expert_out_stored")
        s_left = [sem(f"out_half_{h}_freed") for h in range(2)]
        s_yg = [sem(f"outputs_gathered_{i}") for i in range(T)]
        s_acc, s_out = sem("result_ready"), sem("result_stored")
        block = ctx.enter_context(nc.Block())

        chunks = [(0, 512), (512, 512), (1024, N - 1024)]
        wide = [(0, 512), (512, 512), (1024, NP - 1024)]

        def rows(c):
            return P if c < T - 1 else LAST

        def held(eng, semaphore, value):
            eng.wait_ge(semaphore, value)
            eng.sem_inc(s_pass, 1)

        def each_round(eng, body):
            body(0)
            eng.wait_ge(s_most, 1)
            largest = eng.value_load(most_i[0:1, 0:1], min_val=0, max_val=N)
            with eng.If(largest > CAP):
                with eng.Fori(1, ROUNDS) as r:
                    with eng.If(largest > r * CAP):
                        body(r)

        @block.sync
        def _(sp):
            sp.dma_start(xraw[:, :, :], x.rearrange("(t p) d -> p t d", p=P)).then_inc(s_x, 16)
            for dst, src in ((w1s, w1_t), (w2s, w2_t), (w3s, w3_t), (cs, consts),
                             (wrs, wr), (brs, br)):
                sp.dma_start(dst[:, :], src).then_inc(s_w, 16)
            sp.dma_start(us[:, :, :], u_t.rearrange("(u d) o -> d u o", d=D)).then_inc(s_w, 16)
            sp.dma_start(adj[:, 0:T - 1, :], adj_t[0:(T - 1) * P, :].rearrange("(t p) n -> p t n", p=P)).then_inc(s_adj, 16)
            sp.dma_start(adj[0:LAST, T - 1, :], adj_t[(T - 1) * P:N, :]).then_inc(s_adj, 16)
            sp.wait_ge(s_zero, 1)
            sp.dma_start(slot_x.rearrange("(p k) d -> p (k d)", p=P), zero).then_inc(s_zeroed, 16)
            sp.wait_ge(s_tp, 5)
            sp.dma_start(xraw[:, :, :], x.rearrange("(t p) d -> p t d", p=P)).then_inc(s_xr, 16)
            for dst, src in ((gs, ln_g), (bs, ln_b), (eb1s, eb1), (eb2s, eb2)):
                sp.dma_start(dst, src).then_inc(s_xr, 16)

            def body(r):
                def group(g):
                    for s in range(SLOTS):
                        e = g * SLOTS + s
                        sp.wait_ge(s_y, r * E + e + 1)
                        sp.dma_start(rw1[:, s, :], ew1[bass.ds(e * D, D), :]).then_inc(s_wl[s], 16)
                        sp.dma_start(rw2[:, s, :, :], ew2[bass.ds(e * F, F), :].rearrange("(c p) d -> p c d", p=P)).then_inc(s_wl[s], 16)
                with sp.Fori(0, GROUPS) as g:
                    group(g)
            each_round(sp, body)
            sp.wait_ge(s_acc, 1)
            sp.dma_start(out[0:(T - 1) * P, :].rearrange("(t p) d -> p t d", p=P), acc[:, 0:T - 1, :]).then_inc(s_out, 16)
            sp.dma_start(out[(T - 1) * P:N, :], acc[0:LAST, T - 1, :]).then_inc(s_out, 16)
            sp.wait_ge(s_out, 32)

        @block.gpsimd
        def _(gp):
            nc.gpsimd.memset(zero, 0.0).then_inc(s_zero, 1)
            gp.iota(column, pattern=[[1, N]], base=0, channel_multiplier=0, allow_small_or_imprecise_dtypes=True).then_inc(s_col, 1)
            gp.wait_ge(s_zeroed, 16)

            def body(r):
                held(gp, s_slot, r + 1)
                for k in range(2):
                    for i in range(T):
                        gp.indirect_dma_start(out=slot_x, out_offset=bass.IndirectOffsetOnAxis(ap=slot_i[:, k, i:i + 1], axis=0),
                                              in_=xn[:, i, :], in_offset=None, bounds_check=E * CAP - 1, oob_is_err=False).then_inc(s_sent, 16)
                for q in range(2 * GROUPS):
                    held(gp, s_yf, r * E + (q + 1) * HALF + 2)
                    gp.dma_start(slot_y[q * HALF * CAP:(q + 1) * HALF * CAP, :].rearrange("(e c) d -> c e d", c=CAP),
                                 ysb[0:CAP, q % 2 * HALF:(q % 2 + 1) * HALF, :]).then_inc(s_ys, 16)
                    gp.wait_ge(s_ys, r * (2 * GROUPS * 16) + (q + 1) * 16)
                    gp.sem_inc(s_left[q % 2], 1)
                for i in range(T):
                    for k in range(2):
                        gp.indirect_dma_start(out=yg[:, k, i, :], out_offset=None, in_=slot_y,
                                              in_offset=bass.IndirectOffsetOnAxis(ap=slot_i[:, k, i:i + 1], axis=0),
                                              bounds_check=E * CAP - 1, oob_is_err=False).then_inc(s_yg[i], 16)
            each_round(gp, body)

        @block.tensor
        def _(pe):
            def transposes(src, which, width=D):
                for i in range(T):
                    last = nc.tensor.transpose(SETS[which][0:width, i * P:(i + 1) * P], src[:, i, 0:width], ident)
                last.then_inc(s_tp, 1)

            pe.wait_ge(s_w, 16 * 7)
            pe.wait_ge(s_norm, 1)
            transposes(f0, 0)
            for n in range(STEPS):
                ta = t_a
                pe.wait_ge(s_te, 1 if n == 0 else 3)
                for c0, w in wide:
                    last = nc.tensor.matmul(SETS[1][0:DA, c0:c0 + w], w1s[:, :], ta[:, c0:c0 + w], start=True, stop=True)
                last.then_inc(s_proj, 1)
                for c0, w in wide:
                    last = nc.tensor.matmul(SETS[0][0:DA, c0:c0 + w], w3s[:, :], ta[:, c0:c0 + w], start=True, stop=True)
                last.then_inc(s_proj, 1)
                pe.wait_ge(s_projc, 3 * n + 1)
                for c0, w in wide:
                    last = nc.tensor.matmul(SETS[1][0:DA, c0:c0 + w], w2s[:, :], t_a2[0:DA, c0:c0 + w], start=True, stop=True)
                last.then_inc(s_proj, 1)
                pe.wait_ge(s_projc, 3 * n + 3)
                for i in range(T):
                    if i >= 2:
                        pe.wait_ge(s_exp[n], i - 1)
                    for c0, w in chunks:
                        last = nc.tensor.matmul(SETS[i % 2][:, c0:c0 + w], q_t[:, i * P:(i + 1) * P], k_t[:, c0:c0 + w], start=True, stop=True)
                    last.then_inc(s_lg[n], 1)
                pe.wait_ge(s_adj, 32)
                if n == 1:
                    pe.wait_ge(s_rs[0], 1)
                fin = f0 if n == 0 else f1
                for i in range(T):
                    if i >= 2:
                        pe.wait_ge(s_rc[n], i - 1)
                    ob = psum[:, 6 + i % 2, 0:D + 1]
                    for c in range(T):
                        nc.tensor.matmul(ob, adj[0:rows(c), c, i * P:(i + 1) * P], fin[0:rows(c), c, 0:D + 1], start=(c == 0), stop=False)
                    nc.tensor.matmul(ob, ident, fin[:, i, 0:D + 1], start=False, stop=True).then_inc(s_r[n], 1)
                pe.wait_ge(s_rc[n], T)
                pe.wait_ge(s_exp[n], T)
                vin = f0 if n == 0 else a1
                for i in range(T + 1):
                    for part, (a, b) in enumerate(PARTS):
                        if i == a:
                            pe.wait_ge(s_flag, n * len(PARTS) + part + 1)
                            if a > 0:
                                pe.wait_ge(s_ptc[n], a)
                            for k in range(2):
                                last = nc.tensor.matmul(counts[:, k, a:b], ones[:, 0:1], both[:, k, a:b], start=True, stop=True)
                            last.then_inc(s_flagsum, 1)
                    if i < T:
                        pe.wait_ge(s_mask[n], i + 1)
                        if i >= 2:
                            pe.wait_ge(s_ptc[n], i - 1)
                        for c in range(T):
                            last = nc.tensor.transpose(SETS[i % 2][0:rows(c), c * P:(c + 1) * P], probs[:, i, c * P:c * P + rows(c)], ident)
                        last.then_inc(s_pt[n], 1)
                    if i >= 1:
                        j = i - 1
                        pe.wait_ge(s_ptc[n], j + 1)
                        if j >= 2:
                            pe.wait_ge(s_ac[n], j - 1)
                        for c in range(T):
                            last = nc.tensor.matmul(psum[:, 6 + j % 2, 0:D], p_t[0:rows(c), j % 2, c, :], vin[0:rows(c), c, 0:D], start=(c == 0), stop=(c == T - 1))
                        last.then_inc(s_a[n], 1)
                pe.wait_ge(s_ac[n], T)
                pe.wait_ge(s_rs[n], 1)
                if n == 0:
                    transposes(f1, 0)
                    transposes(a1, 1)
                    pe.wait_ge(s_te, 3)
                else:
                    transposes(f1, 1)
                    transposes(xraw, 0)
                    pe.wait_ge(s_te, 5)
            nc.tensor.drain().then_inc(s_y, SLOTS)
            for i in range(T):
                if i >= 2:
                    pe.wait_ge(s_hc, i - 1)
                ob = psum[:, 6 + i % 2, 0:D]
                for u, src in enumerate((t_f1, t_f2, t_a, t_a2)):
                    nc.tensor.matmul(ob, src[:, i * P:(i + 1) * P], us[:, u, :], start=(u == 0), stop=False)
                nc.tensor.matmul(ob, ident, f0[:, i, 0:D], start=False, stop=True).then_inc(s_h, 1)
            for c in range(len(BANK_TILES) + 1):
                if c < len(BANK_TILES):
                    pe.wait_ge(s_norm, 2 + c)
                    for i in range(*BANK_TILES[c]):
                        last = nc.tensor.transpose(SETS[0][0:D, i * P:(i + 1) * P], xn[:, i, :], ident)
                    last.then_inc(s_tp, 1)
                if c >= 1:
                    pe.wait_ge(s_te, 5 + c)
                    for i in range(*BANK_TILES[c - 1]):
                        last = nc.tensor.matmul(SETS[1][:, i * E:(i + 1) * E], t_a[:, i * P:(i + 1) * P], wrs[:, :], start=True, stop=True, skip_group_check=True)
            last.then_inc(s_rl, 1)
            pe.wait_ge(s_m, 1)
            for a, b in ((0, BANK // E), (BANK // E, T)):
                ob = SETS[0][:, a * E:b * E]
                nc.tensor.matmul(ob, tri, mm[:, a:b, :], start=True, stop=False)
                nc.tensor.matmul(ob, ones, macc[:, a:b, :], start=False, stop=True)
            nc.tensor.matmul(SETS[0][:, T * E:(T + 1) * E], ones, macc[:, T, :], start=True, stop=True).then_inc(s_rk, 1)
            pe.wait_ge(s_cb, 1)
            pe.wait_ge(s_rlc, 1)
            for i in range(T):
                last = nc.tensor.transpose(SETS[1][0:E, i * P:(i + 1) * P], comb[:, i, :], ident)
            last.then_inc(s_cbt, 1)
            pe.wait_ge(s_cbtc, 1)
            pe.wait_ge(s_rkc, 1)
            for i in range(T):
                last = nc.tensor.matmul(SETS[0][:, i * D:(i + 1) * D], comb_t[:, i * P:(i + 1) * P], eb2s, start=True, stop=True)
            last.then_inc(s_b2, 1)

            def body(r):
                for b in range(E // 4):
                    if b * 4 % SLOTS == 0:
                        held(pe, s_xg[b * 4 // SLOTS], (r + 1) * 16)
                    pe.wait_ge(s_xtf, r * (E // 4) + b + 1)
                    for k in range(4):
                        last = nc.tensor.transpose(psum[:, b % 2, k * CAP:(k + 1) * CAP], xg[:, 4 * b + k, :], ident[0:CAP, 0:CAP])
                    last.then_inc(s_xt, 1)
                held(pe, s_xtf, (r + 1) * (E // 4) + 2)

                def first(e, s, loads):
                    held(pe, s_wl[s], 32 * (r * GROUPS + loads))
                    pe.wait_ge(s_hf, r * E + e + 1)
                    for c in range(FC):
                        last = nc.tensor.matmul(psum[:, 2 + s % 2, c * CAP:(c + 1) * CAP], rw1[:, s, c * P:(c + 1) * P],
                                                xgt[:, bass.ds(e, 1), :], start=True, stop=True)
                    last.then_inc(s_hp, 1)

                def second(e, s):
                    pe.wait_ge(s_hf, r * E + e + 3)
                    pe.wait_ge(s_yf, r * E + e + 1)
                    for c in range(FC):
                        last = nc.tensor.matmul(psum[0:CAP, 4 + s % 2, 0:D], hid[:, s % 2, c, 0:CAP], rw2[:, s, c, :],
                                                start=(c == 0), stop=(c == FC - 1))
                    last.then_inc(s_y, 1)

                first(0, 0, 1)
                with pe.Fori(0, GROUPS - 1) as g:
                    for s in range(SLOTS):
                        first(g * SLOTS + s + 1, (s + 1) % SLOTS, g + (1 if s < SLOTS - 1 else 2))
                        second(g * SLOTS + s, s)
                for s in range(SLOTS):
                    if s < SLOTS - 1:
                        first(E - SLOTS + s + 1, s + 1, GROUPS)
                    second(E - SLOTS + s, s)
            each_round(pe, body)

        @block.scalar
        def _(act):
            def std(k):
                act.wait_ge(s_var, k)
                nc.scalar.activation(rstd[:, :], rstd[:, :], ACT.Sqrt).then_inc(s_std, 1)

            def copy_out(dst, which, k, width=D):
                act.wait_ge(s_tp, k)
                nc.scalar.activation(dst[0:width, :], SETS[which][0:width, 0:NP], ACT.Copy).then_inc(s_te, 1)

            std(1)
            copy_out(t_a, 0, 1)
            for n in range(STEPS):
                tmid = t_a2[0:DA, :]
                for k, (dst, which) in enumerate(((tmid, 1), (k_t[:, :], 0), (q_t[:, :], 1))):
                    act.wait_ge(s_proj, 3 * n + k + 1)
                    nc.scalar.activation(dst, SETS[which][0:DA, 0:NP], ACT.Copy).then_inc(s_projc, 1)
                if n == 0:
                    act.wait_ge(s_zeroed, 16)
                for i in range(T):
                    act.wait_ge(s_neg[n], i + 1)
                    nc.scalar.activation(probs[:, i, :], SETS[i % 2][:, 0:N], ACT.Exp, bias=negmax[:, i:i + 1],
                                         accum_out=zsum[:, i:i + 1])
                    nc.scalar.activation(cand[:, i, 0:8 * CHUNKS[n]], cand[:, i, 0:8 * CHUNKS[n]], ACT.Exp, bias=negmax[:, i:i + 1]).then_inc(s_exp[n], 1)
                rdst = f1 if n == 0 else xraw
                for i in range(T):
                    act.wait_ge(s_r[n], i + 1)
                    if n == 0:
                        nc.scalar.activation(rrow[:, i:i + 1], psum[:, 6 + i % 2, D:D + 1], ACT.Copy)
                    nc.scalar.activation(rdst[:, i, 0:D], psum[:, 6 + i % 2, 0:D], ACT.Copy).then_inc(s_rc[n], 1)
                adst = a1 if n == 0 else f1
                for i in range(T + 1):
                    if i < T:
                        act.wait_ge(s_pt[n], i + 1)
                        if i >= 2:
                            act.wait_ge(s_a[n], i - 1)
                        pt = p_t[:, i % 2, :, :].rearrange("p t n -> p (t n)")
                        nc.scalar.activation(pt[:, 0:NP - P], SETS[i % 2][:, 0:NP - P], ACT.Copy)
                        nc.scalar.activation(pt[0:LAST, NP - P:NP], SETS[i % 2][0:LAST, NP - P:NP], ACT.Copy).then_inc(s_ptc[n], 1)
                    if i >= 1:
                        j = i - 1
                        act.wait_ge(s_a[n], j + 1)
                        act.wait_ge(s_scale[n], j + 1)
                        nc.scalar.activation(adst[:, j, 0:D], psum[:, 6 + j % 2, 0:D], ACT.Copy, scale=rkept[:, j:j + 1]).then_inc(s_ac[n], 1)
                if n == 0:
                    copy_out(t_f1, 0, 2)
                    copy_out(t_a, 1, 3)
                else:
                    copy_out(t_a2, 1, 4)
                    copy_out(t_f2, 0, 5)
            for i in range(T):
                act.wait_ge(s_h, i + 1)
                nc.scalar.activation(hrow[:, i, :], psum[:, 6 + i % 2, 0:D], ACT.Copy).then_inc(s_hc, 1)
            std(2)
            std(3)
            for c, (a, b) in enumerate(BANK_TILES):
                act.wait_ge(s_tp, 6 + c)
                nc.scalar.activation(t_a[:, a * P:b * P], SETS[0][:, a * P:b * P], ACT.Copy).then_inc(s_te, 1)
            act.wait_ge(s_gd, 1)
            nc.scalar.activation(gexp, gdiff, ACT.Exp).then_inc(s_ge, 1)
            act.wait_ge(s_cbt, 1)
            nc.scalar.activation(comb_t[:, :], SETS[1][0:E, 0:NP], ACT.Copy).then_inc(s_cbtc, 1)
            nc.scalar.drain().then_inc(s_hf, 2)
            nc.scalar.drain().then_inc(s_left[0], 1)
            nc.scalar.drain().then_inc(s_left[1], 1)

            def body(r):
                held(act, s_sent, (r + 1) * (2 * T * 16))
                for q in range(GROUPS):
                    act.dma_start(xg[:, q * SLOTS:(q + 1) * SLOTS, :],
                                  slot_x[q * SLOTS * CAP:(q + 1) * SLOTS * CAP, :].rearrange("(e c) d -> c e d", c=CAP)).then_inc(s_xg[q], 16)

                def group(g):
                    for s in range(SLOTS):
                        e = g * SLOTS + s
                        act.wait_ge(s_hp, r * E + e + 1)
                        if s >= 2:
                            act.wait_ge(s_y, SLOTS + r * E + e - 1)
                        for c in range(FC):
                            last = nc.scalar.activation(hid[:, s % 2, c, 0:CAP], psum[:, 2 + s % 2, c * CAP:(c + 1) * CAP], ACT.Relu,
                                                        bias=eb1s[:, bass.ds(e * FC + c, 1)])
                        last.then_inc(s_hf, 1)
                with act.Fori(0, GROUPS) as g:
                    group(g)
            each_round(act, body)

        @block.vector
        def _(dve):
            V = nc.vector

            def settle():
                V.drain()

            def aggregate():
                settle()
                for i in range(T):
                    V.bn_aggr(mv[:, i, :], stats[:, i, :])
                settle()
                V.tensor_scalar(rstd[:, :], mv[:, :, 1], EPS, None, ALU.add).then_inc(s_var, 1)

            def invert_std(k):
                dve.wait_ge(s_std, k)
                V.reciprocal(rstd[:, :], rstd[:, :])
                settle()

            def variance(src, k):
                for i in range(T):
                    V.bn_stats(stats[:, i, :], src(i))
                aggregate()
                invert_std(k)

            def normalise(src, dst, k):
                variance(src, k)
                for i in range(T):
                    V.tensor_scalar(dst(i), src(i), mv[:, i, 0:1], rstd[:, i:i + 1], ALU.subtract, ALU.mult)
                settle()

            V.memset(f0[:, :, D:D + 1], 1.0)
            dve.wait_ge(s_x, 16)
            normalise(lambda i: xraw[:, i, :], lambda i: f0[:, i, 0:D], 1)
            V.memset(f1[:, :, D:D + 1], 1.0)
            V.drain().then_inc(s_norm, 1)

            def cumulate(a, b, eight):
                for j in range(8):
                    V.tensor_tensor(cum[:, a:b, j + 1], cum[:, a:b, j], eight[:, :, j], ALU.add)
                    settle()

            def update(a, b):
                V.tensor_tensor(yes[:, a:b], mass[:, a:b], target[:, a:b], ALU.is_lt)
                V.tensor_tensor(no[:, a:b], mass[:, a:b], target[:, a:b], ALU.is_ge)
                settle()
                V.copy_predicated(hi[:, a:b], yes[:, a:b], mid[:, a:b])
                V.copy_predicated(above[:, a:b], yes[:, a:b], mass[:, a:b])
                V.copy_predicated(lo[:, a:b], no[:, a:b], mid[:, a:b])
                settle()

            def row_mass(i):
                V.scalar_tensor_tensor(out=below[:, :], in0=probs[:, i, :], scalar=mid[:, i:i + 1], in1=probs[:, i, :],
                                       op0=ALU.is_ge, op1=ALU.mult, accum_out=mass[:, i:i + 1])
                settle()

            def halve_row(i):
                lo_i, hi_i, mid_i = (a[:, i:i + 1].bitcast(I32) for a in (lo, hi, mid))
                V.tensor_tensor(low_i[:, i:i + 1], lo_i, hi_i, ALU.bitwise_xor)
                V.tensor_tensor(high_i[:, i:i + 1], lo_i, hi_i, ALU.bitwise_and)
                settle()
                V.tensor_scalar(low_i[:, i:i + 1], low_i[:, i:i + 1], 1, None, ALU.arith_shift_right)
                settle()
                V.tensor_tensor(mid_i, low_i[:, i:i + 1], high_i[:, i:i + 1], ALU.add)
                settle()
                row_mass(i)
                update(i, i + 1)

            def read_cut(a, b, to, eight, d, w):
                V.tensor_copy(cum[:, a:b, 0], above[:, a:b])
                settle()
                cumulate(a, b, eight)
                V.tensor_tensor(d, cum[:, a:b, 0:8], target[:, a:b].unsqueeze(2).broadcast_to([P, b - a, 8]), ALU.is_ge)
                settle()
                V.scalar_tensor_tensor(out=w, in0=d, scalar=4.0, in1=eight, op0=ALU.mult, op1=ALU.add)
                settle()
                V.tensor_reduce(to[:, a:b], w, axis=AX.X, op=ALU.min)
                settle()
                V.tensor_tensor(w, d, eight, ALU.mult)
                settle()
                V.tensor_reduce(mass[:, a:b], w, axis=AX.X, op=ALU.max)
                settle()
                V.tensor_tensor(mass[:, a:b], mass[:, a:b], to[:, a:b], ALU.is_ge)
                V.tensor_scalar(flags[:, a:b], d[:, :, 7], -1.0, 1.0, ALU.mult, ALU.add)
                settle()

            def any_flag(flags, a, b):
                V.tensor_reduce(flag32[:, 0:1], flags[:, a:b], axis=AX.X, op=ALU.max)
                settle()
                V.transpose(flag32t[:, :], flag32[:, :])
                settle()
                V.tensor_reduce(flag1[:, :], flag32t[:, :], axis=AX.X, op=ALU.max)
                settle()
                V.tensor_copy(flag_i[:, :], flag1[:, :])
                settle()
                four = [dve.value_load(flag_i[q:q + 1, 0:1], min_val=0, max_val=2) for q in range(0, P, 32)]
                return four[0] + four[1] + four[2] + four[3]

            def exact_row(i, scan):
                one = slice(i, i + 1)
                V.tensor_scalar(lo[:, one], zsum[:, one], (1.0 - TOP_P) / (2 * N), None, ALU.mult)
                V.memset(hi[:, one], 2.0)
                V.memset(above[:, one], 0.0)
                settle()
                with dve.Fori(0, EXACT):
                    halve_row(i)
                V.tensor_copy(cut[:, one], lo[:, one])
                V.tensor_tensor(mass[:, one], target[:, one], above[:, one], ALU.subtract)
                V.reciprocal(kept[:, one], lo[:, one])
                settle()
                V.tensor_tensor(mass[:, one], mass[:, one], kept[:, one], ALU.mult)
                settle()
                V.tensor_scalar(mass[:, one], mass[:, one], 1.0, None, ALU.add)
                V.tensor_scalar(below[:, :], probs[:, i, :], cut[:, one], None, ALU.is_equal)
                settle()
                V.tensor_tensor_scan(scan, below[:, :], below[:, :], 0.0, ALU.add, ALU.max)
                settle()
                V.tensor_tensor(below[:, :], below[:, :], scan, ALU.mult)
                settle()
                V.scalar_tensor_tensor(out=probs[:, i, :], in0=below[:, :], scalar=mass[:, one], in1=probs[:, i, :],
                                       op0=ALU.is_lt, op1=ALU.mult)
                V.memset(ties[:, one], 0.0)
                settle()

            def retry_row(i, scan):
                one = slice(i, i + 1)
                V.tensor_copy(opened[:, :], flags[:, one])
                V.tensor_tensor(yes[:, one], hidden[:, one], cut[:, one], ALU.is_ge)
                V.memset(redone[:, 0, 0:1], 2.0)
                V.memset(redone[:, 0, 1:2], 0.0)
                V.tensor_scalar(mid[:, one], hidden[:, one], 1.0 + 2.0 ** -20, None, ALU.mult)
                settle()
                V.copy_predicated(hi[:, one], yes[:, one], redone[:, 0, 0:1])
                V.copy_predicated(above[:, one], yes[:, one], redone[:, 0, 1:2])
                V.tensor_tensor(mid[:, one], mid[:, one], lo[:, one], ALU.max)
                settle()
                row_mass(i)
                update(i, i + 1)
                with dve.Fori(0, RETRY):
                    halve_row(i)
                V.scalar_tensor_tensor(out=below[:, :], in0=probs[:, i, :], scalar=hi[:, one], in1=probs[:, i, :],
                                       op0=ALU.is_lt, op1=ALU.mult)
                settle()
                V.max(retop[:, 0, :], below[:, :])
                settle()
                read_cut(i, i + 1, found, retop[:, :, :], redone[:, :, :], work8[:, i:i + 1, :])
                V.copy_predicated(cut[:, one], opened[:, :], found[:, one])
                V.copy_predicated(ties[:, one], opened[:, :], mass[:, one])
                V.copy_predicated(etop[:, i, :], opened[:, :].broadcast_to([P, 8]), retop[:, 0, :])
                V.copy_predicated(done8[:, i, :], opened[:, :].broadcast_to([P, 8]), redone[:, 0, :])
                V.tensor_tensor(flags[:, one], flags[:, one], opened[:, :], ALU.mult)
                settle()
                with dve.If(any_flag(flags, i, i + 1) > 0):
                    exact_row(i, scan)

            V.memset(flag32[:, :], 0.0)
            V.memset(one_i[:, :], 1)
            dve.wait_ge(s_col, 1)
            for n in range(STEPS):
                width, chunk_count = WIDTH[n], CHUNKS[n]
                cands = 8 * chunk_count
                for i in range(T):
                    dve.wait_ge(s_lg[n], i + 1)
                    for c in range(chunk_count):
                        V.max(cand[:, i, 8 * c:8 * c + 8], SETS[i % 2][:, c * width:(N if c == chunk_count - 1 else (c + 1) * width)])
                    settle()
                    V.tensor_reduce(negmax[:, i:i + 1], cand[:, i, 0:cands:8], axis=AX.X, op=ALU.max)
                    settle()
                    V.tensor_scalar(negmax[:, i:i + 1], negmax[:, i:i + 1], -1.0, None, ALU.mult).then_inc(s_neg[n], 1)
                for part, (a, b) in enumerate(PARTS):
                    dve.wait_ge(s_exp[n], b)
                    V.tensor_scalar(target[:, a:b], zsum[:, a:b], TOP_P, None, ALU.mult)
                    V.tensor_scalar(lo[:, a:b], zsum[:, a:b], (1.0 - TOP_P) / (2 * N), None, ALU.mult)
                    V.memset(hi[:, a:b], 2.0)
                    V.memset(above[:, a:b], 0.0)
                    V.tensor_reduce(hidden[:, a:b], cand[:, a:b, 7:cands:8], axis=AX.X, op=ALU.max)
                    settle()
                    for k in range(STEPS_OF_CUT[n]):
                        V.tensor_scalar(mid[:, a:b], lo[:, a:b], 2.0 ** (RANGE / 2 ** (k + 1)), None, ALU.mult)
                        settle()
                        for i in range(a, b):
                            V.scalar_tensor_tensor(out=junk[:, i - a, 0:cands], in0=cand[:, i, 0:cands], scalar=mid[:, i:i + 1], in1=cand[:, i, 0:cands],
                                                   op0=ALU.is_ge, op1=ALU.mult, accum_out=mass[:, i:i + 1])
                        settle()
                        update(a, b)
                    for j in range(a, b, 2):
                        pair = range(j, min(j + 2, b))
                        for i in pair:
                            V.scalar_tensor_tensor(out=picked[:, i % 2, 0:cands], in0=cand[:, i, 0:cands], scalar=hi[:, i:i + 1], in1=cand[:, i, 0:cands],
                                                   op0=ALU.is_lt, op1=ALU.mult)
                        settle()
                        for i in pair:
                            V.max(etop[:, i, :], picked[:, i % 2, 0:cands])
                        settle()
                    read_cut(a, b, cut, etop[:, a:b, :], done8[:, a:b, :], work8[:, a:b, :])
                    V.tensor_copy(ties[:, a:b], mass[:, a:b])
                    settle()
                    V.tensor_tensor(mass[:, a:b], hidden[:, a:b], cut[:, a:b], ALU.is_ge)
                    settle()
                    V.tensor_tensor(flags[:, a:b], flags[:, a:b], mass[:, a:b], ALU.max).then_inc(s_flag, 1)
                    dve.wait_ge(s_flagsum, n * len(PARTS) + part + 1)
                    sums = counts[:, :, a:b]
                    V.tensor_copy(both_i[:, :, a:b], sums)
                    V.tensor_reduce(some[:, :], sums, axis=AX.X, op=ALU.add)
                    settle()
                    V.tensor_copy(some_i[:, :], some[:, :])
                    settle()
                    opens = dve.value_load(some_i[0:1, 0:1], min_val=0, max_val=NP)
                    tied = dve.value_load(some_i[0:1, 1:2], min_val=0, max_val=NP)
                    scan = cand[:, a:b, :].rearrange("p t c -> p (t c)")[:, 0:N]
                    with dve.If(opens > 0):
                        for i in range(a, b):
                            with dve.If(dve.value_load(both_i[0:1, 0, i:i + 1], min_val=0, max_val=P) > 0):
                                retry_row(i, scan)
                    def scale_of(i):
                        if i >= a:
                            V.scalar_tensor_tensor(out=kept[:, i:i + 1], in0=zsum[:, i:i + 1], scalar=1e-12, in1=kept[:, i:i + 1], op0=ALU.mult, op1=ALU.max)
                        if i >= a + 1:
                            V.reciprocal(rkept[:, i - 1:i], kept[:, i - 1:i]).then_inc(s_scale[n], 1)

                    def last_scales():
                        settle()
                        scale_of(b - 1)
                        settle()
                        V.reciprocal(rkept[:, b - 1:b], kept[:, b - 1:b]).then_inc(s_scale[n], 1)

                    with dve.If(tied > 0):
                        V.tensor_tensor(high_i[:, a:b], cut[:, a:b].bitcast(I32), one_i[:, a:b], ALU.add)
                        V.tensor_tensor(last7[:, a:b, :], done8[:, a:b, 1:8], done8[:, a:b, 0:7], ALU.subtract)
                        settle()
                        V.tensor_tensor(lo[:, a:b], high_i[:, a:b].bitcast(F32), cut[:, a:b], ALU.subtract)
                        settle()
                        V.tensor_tensor(lo[:, a:b], lo[:, a:b], ties[:, a:b], ALU.mult)
                        for i in range(a, b):
                            V.max_index(place[:, i, :], etop[:, i, :], probs[:, i, :])
                        settle()
                        V.tensor_copy(work8[:, a:b, :], place[:, a:b, :])
                        settle()
                        V.tensor_tensor(work8[:, a:b, 0:7], work8[:, a:b, 0:7], last7[:, a:b, :], ALU.mult)
                        settle()
                        V.tensor_reduce(mid[:, a:b], work8[:, a:b, 0:7], axis=AX.X, op=ALU.add)
                        settle()
                        def raise_cut(i):
                            V.tensor_scalar(raised, column, mid[:, i:i + 1], lo[:, i:i + 1], ALU.is_gt, ALU.mult)

                        raise_cut(a)
                        for i in range(a, b):
                            settle()
                            V.scalar_tensor_tensor(out=below[:, :], in0=raised, scalar=cut[:, i:i + 1], in1=probs[:, i, :],
                                                   op0=ALU.add, op1=ALU.is_le)
                            scale_of(i - 1)
                            settle()
                            V.scalar_tensor_tensor(out=probs[:, i, :], in0=below[:, :], scalar=1.0, in1=probs[:, i, :],
                                                   op0=ALU.mult, op1=ALU.mult, accum_out=kept[:, i:i + 1]).then_inc(s_mask[n], 1)
                            if i + 1 < b:
                                raise_cut(i + 1)
                        last_scales()
                    with dve.Else():
                        for i in range(a, b):
                            V.scalar_tensor_tensor(out=probs[:, i, :], in0=probs[:, i, :], scalar=cut[:, i:i + 1], in1=probs[:, i, :],
                                                   op0=ALU.is_ge, op1=ALU.mult, accum_out=kept[:, i:i + 1]).then_inc(s_mask[n], 1)
                            scale_of(i - 1)
                            settle()
                        last_scales()
                dve.wait_ge(s_rc[n], T)
                if n == 0:
                    V.reciprocal(rinv[:, :], rrow[:, :])
                    settle()
                rdst = f1[:, :, 0:D] if n == 0 else xraw[:, :, :]
                V.tensor_tensor(rdst, rdst, rinv[:, :].unsqueeze(2).broadcast_to([P, T, D]), ALU.mult).then_inc(s_rs[n], 1)

            dve.wait_ge(s_xr, 16 * 5)
            V.tensor_tensor(xraw[:, :, :], xraw[:, :, :], bs[:, :].unsqueeze(1).broadcast_to([P, T, D]), ALU.add)
            for i in range(T):
                dve.wait_ge(s_hc, i + 1)
                V.bn_stats(stats[:, i, :], hrow[:, i, :])
            dve.wait_ge(s_h, T)
            aggregate()
            for i in range(T):
                V.scalar_tensor_tensor(out=tmp[:, i, :], in0=hrow[:, i, :], scalar=mv[:, i, 0:1], in1=gs[:, :], op0=ALU.subtract, op1=ALU.mult)
            invert_std(2)
            for i in range(T):
                V.scalar_tensor_tensor(out=x1[:, i, :], in0=tmp[:, i, :], scalar=rstd[:, i:i + 1], in1=xraw[:, i, :], op0=ALU.mult, op1=ALU.add)
            settle()
            variance(lambda i: x1[:, i, :], 3)
            for a, b in BANK_TILES:
                for i in range(a, b):
                    V.tensor_scalar(xn[:, i, :], x1[:, i, :], mv[:, i, 0:1], rstd[:, i:i + 1], ALU.subtract, ALU.mult)
                V.drain().then_inc(s_norm, 1)
            V.memset(yg, 0.0)
            V.memset(macc[:, 0, :], 0.0)
            dve.wait_ge(s_rl, 1)
            V.tensor_tensor(lg, SETS[1][:, 0:T * E].rearrange("p (t e) -> p t e", t=T), brs[:, :].unsqueeze(1).broadcast_to([P, T, E]), ALU.add).then_inc(s_rlc, 1)
            settle()
            for i in range(T):
                V.max(top[:, i, :], lg[:, i, :])
            settle()
            for i in range(T):
                V.max_index(idx8[:, i, :], top[:, i, :], lg[:, i, :])
            V.tensor_tensor(gdiff, top[:, :, 1], top[:, :, 0], ALU.subtract).then_inc(s_gd, 1)
            settle()
            for k in range(2):
                V.tensor_copy(eidx[:, k, :], idx8[:, :, k])
            settle()
            for k, m in enumerate((m1, m2)):
                V.tensor_tensor(m, iota.unsqueeze(1).broadcast_to([P, T, E]), eidx[:, k, :].unsqueeze(2).broadcast_to([P, T, E]), ALU.is_equal)
            settle()
            for m in (m1, m2):
                V.tensor_scalar(m[:, T - 1, :], m[:, T - 1, :], real, None, ALU.mult)
            settle()
            V.tensor_tensor(mm, m1, m2, ALU.add)
            settle()
            V.tensor_copy(macc[:, 1, :], mm[:, 0, :])
            settle()
            for i in range(1, T):
                V.tensor_tensor(macc[:, i + 1, :], macc[:, i, :], mm[:, i, :], ALU.add)
                settle()
            V.drain().then_inc(s_m, 1)
            dve.wait_ge(s_rk, 1)
            V.tensor_copy(ranks, SETS[0][:, 0:T * E].rearrange("p (t e) -> p t e", t=T))
            V.tensor_reduce(most, SETS[0][:, T * E:(T + 1) * E], axis=AX.X, op=ALU.max)
            settle()
            V.tensor_copy(most_i, most)
            V.drain().then_inc(s_rkc, 1)
            V.drain().then_inc(s_most, 1)
            for k, m in enumerate((m1, m2)):
                V.tensor_tensor(prod, ranks, m, ALU.mult)
                settle()
                V.tensor_reduce(rank[:, k, :], prod, axis=AX.X, op=ALU.add)
                settle()
            V.tensor_scalar(flag1[:, :], real, -FAR, FAR, ALU.mult, ALU.add)
            settle()
            for k in range(2):
                V.tensor_scalar(rank[:, k, T - 1:T], rank[:, k, T - 1:T], flag1[:, 0:1], None, ALU.add)
            V.tensor_scalar(base[:, :, :], eidx[:, :, :], float(CAP), -FAR, ALU.mult, ALU.add)
            settle()
            def first_sum():
                dve.wait_ge(s_ge, 1)
                V.tensor_scalar(gdiff, gexp, 1.0, None, ALU.add)
                settle()
                V.reciprocal(gate[:, 0, :], gdiff)
                settle()
                V.tensor_tensor(gate[:, 1, :], gexp, gate[:, 0, :], ALU.mult)
                settle()
                V.tensor_tensor(comb, m1, gate[:, 0, :].unsqueeze(2).broadcast_to([P, T, E]), ALU.mult)
                V.tensor_tensor(prod, m2, gate[:, 1, :].unsqueeze(2).broadcast_to([P, T, E]), ALU.mult)
                settle()
                V.tensor_tensor(comb, comb, prod, ALU.add)
                V.drain().then_inc(s_cb, 1)
                dve.wait_ge(s_b2, 1)
                V.tensor_tensor(acc[:, :, :], SETS[0][:, 0:NP].rearrange("p (t d) -> p t d", t=T), x1, ALU.add)
                settle()
                V.drain().then_inc(s_xtf, 2)
                V.drain().then_inc(s_yf, 2)


            def body(r):
                V.tensor_scalar(ok1[:, :, :], rank[:, :, :], 0.0, None, ALU.is_ge)
                V.tensor_scalar(ok2[:, :, :], rank[:, :, :], float(CAP), None, ALU.is_lt)
                V.tensor_tensor(slot[:, :, :], base[:, :, :], rank[:, :, :], ALU.add)
                settle()
                V.tensor_tensor(ok1[:, :, :], ok1[:, :, :], ok2[:, :, :], ALU.mult)
                settle()
                V.tensor_tensor(slot[:, :, :], slot[:, :, :], ok1[:, :, :], ALU.mult)
                settle()
                V.tensor_scalar(slot_i[:, :, :], slot[:, :, :], FAR, None, ALU.add)
                V.tensor_scalar(rank[:, :, :], rank[:, :, :], float(-CAP), None, ALU.add)
                if not isinstance(r, int):
                    V.memset(yg, 0.0)
                V.drain().then_inc(s_slot, 1)
                if isinstance(r, int):
                    first_sum()
                for b in range(E // 4):
                    dve.wait_ge(s_xt, r * (E // 4) + b + 1)
                    V.tensor_copy(xgt[:, 4 * b:4 * b + 4, :], psum[:, b % 2, 0:4 * CAP].rearrange("p (e c) -> p e c", e=4)).then_inc(s_xtf, 1)

                def group(g):
                    for s in range(SLOTS):
                        if s % HALF == 0:
                            dve.wait_ge(s_left[s // HALF], r * GROUPS + g + 1)
                        e = g * SLOTS + s
                        dve.wait_ge(s_y, SLOTS + r * E + e + 1)
                        V.tensor_copy(ysb[0:CAP, s, :], psum[0:CAP, 4 + s % 2, 0:D]).then_inc(s_yf, 1)
                with dve.Fori(0, GROUPS) as g:
                    group(g)
                for i in range(T):
                    dve.wait_ge(s_yg[i], (r + 1) * (2 * 16))
                    for k in range(2):
                        V.scalar_tensor_tensor(out=acc[:, i, :], in0=yg[:, k, i, :], scalar=gate[:, k, i:i + 1], in1=acc[:, i, :], op0=ALU.mult, op1=ALU.add)
                        settle()
            each_round(dve, body)
            V.drain().then_inc(s_acc, 1)


def kernel(x, adj, L0_gnn_W1, L0_gnn_W2, L0_gnn_W3, L0_gnn_U1, L0_gnn_U2, L0_gnn_ln_g, L0_gnn_ln_b,
           L0_ffn_Wr, L0_ffn_br, L0_ffn_W1, L0_ffn_b1, L0_ffn_W2, L0_ffn_b2):
    import numpy as np
    import concourse.bacc as bacc
    from concourse.bass_utils import run_bass_kernel_spmd

    f = np.float32
    pad = NP - N
    consts = np.concatenate([np.eye(P, dtype=f), np.triu(np.ones((P, P), f), 1), np.ones((P, P), f),
                             np.broadcast_to(np.arange(E, dtype=f), (P, E)),
                             (np.arange(P) < LAST).astype(f)[:, None]], axis=1)
    adj = np.asarray(adj)
    x = np.asarray(x)
    arrays = {
        "x": np.concatenate([x, x[:pad]], axis=0),
        "adj_t": np.concatenate([adj.T, adj.T[:, :pad]], axis=1),
        "w1_t": np.asarray(L0_gnn_W1).T,
        "w2_t": np.asarray(L0_gnn_W2).T,
        "w3_t": np.asarray(L0_gnn_W3).T,
        "u_t": np.concatenate([np.asarray(u)[n].T for u in (L0_gnn_U1, L0_gnn_U2) for n in range(STEPS)], axis=0),
        "ln_g": np.broadcast_to(np.asarray(L0_gnn_ln_g), (P, D)),
        "ln_b": np.broadcast_to(np.asarray(L0_gnn_ln_b), (P, D)),
        "wr": np.asarray(L0_ffn_Wr),
        "br": np.broadcast_to(np.asarray(L0_ffn_br), (P, E)),
        "ew1": np.asarray(L0_ffn_W1).reshape(E * D, F),
        "eb1": np.asarray(L0_ffn_b1).reshape(E * FC, P).T,
        "ew2": np.asarray(L0_ffn_W2).reshape(E * F, D),
        "eb2": np.asarray(L0_ffn_b2),
        "consts": consts,
    }
    nc = bacc.Bacc("TRN2", target_bir_lowering=False, num_devices=1)
    arrays = {f"in_{k}": np.ascontiguousarray(v) for k, v in arrays.items()}
    args = [nc.dram_tensor(k, v.shape, mybir.dt.from_np(v.dtype), kind="ExternalInput").ap() for k, v in arrays.items()]
    out = nc.dram_tensor("out_0", (N, D), mybir.dt.float32, kind="ExternalOutput").ap()
    build(nc, *args, out)
    return run_bass_kernel_spmd(nc, [arrays], core_ids=[0]).results[0]["out_0"]
```

```python
import math
from contextlib import ExitStack

import concourse.bass as bass
from concourse import mybir

P = 128
N = 1354
D = 128
DA = 64
STEPS = 2
TOP_P = 0.9
EPS = 1e-5
T = -(-N // P)
NP = T * P
LAST = N - (T - 1) * P
E = 64
F = 256
FC = F // P
CAP = 96
ROUNDS = -(-N // CAP)
SLOTS = 16
GROUPS = E // SLOTS
HALF = SLOTS // 2
WIDTH = (113, 25)
CHUNKS = tuple(N // w for w in WIDTH)
RANGE = math.log2(2 * N / (1.0 - TOP_P)) + 0.1
STEPS_OF_CUT = (5, 10)
RETRY = 6
PARTS = (((0, 7), (7, T)), ((0, 5), (5, T)))
BETWEEN = ([[i // 2 - 3] if i in (6, 8, 10) else [] for i in range(T)], [[i - 1] if i else [] for i in range(T)])
EXACT = 32
BANK = 512
NB = -(-T * P // BANK)
BANK_TILES = [(t, min(t + BANK // P, T)) for t in range(0, T, BANK // P)]
FAR = float(E * CAP * 2)


def build(nc, x, adj_t, w1_t, w2_t, w3_t, u_t, ln_g, ln_b, wr, br, ew1, eb1, ew2, eb2, consts, out):
    BF16 = mybir.dt.bfloat16
    F32, I32, U32 = mybir.dt.float32, mybir.dt.int32, mybir.dt.uint32
    ALU = mybir.AluOpType
    ACT = mybir.ActivationFunctionType
    AX = mybir.AxisListType

    slot_x = nc.dram_tensor("slot_x", [E * CAP, D], F32, kind="Internal").ap()
    slot_y = nc.dram_tensor("slot_y", [E * CAP, D], F32, kind="Internal").ap()

    with ExitStack() as ctx:
        def sb(name, shape, dt=F32):
            return ctx.enter_context(nc.sbuf_tensor(name, shape, dt))

        def sem(name):
            return ctx.enter_context(nc.semaphore(name))

        adj = sb("adj", [P, T, NP])
        probs = sb("probs", [P, T, N])
        xraw = sb("xraw", [P, T, D])
        f0 = sb("f0", [P, T, D + 1])
        f1 = sb("f1", [P, T, D + 1])
        a1 = sb("a1", [P, T, D])
        t_a = sb("t_a", [P, NP])
        t_a2 = sb("t_a2", [P, NP])
        t_f1 = sb("t_f1", [P, NP])
        t_f2 = sb("t_f2", [P, NP])
        p_t = sb("p_t", [P, 2, T, P])
        rrx_t = p_t[:, 1, :, :].rearrange("p t n -> p (t n)")
        q_k = [p_t[:, b, :, :].rearrange("p t n -> p (t n)") for b in range(2)]
        q_t, k_t = (p_t[0:DA, b, :, :].rearrange("p t n -> p (t n)") for b in range(2))
        below = t_a2[:, 0:N]
        cand = sb("cand", [P, T, 8 * max(CHUNKS)])
        picked = below[:, 0:2 * 8 * max(CHUNKS)].rearrange("p (b c) -> p b c", b=2)
        column = t_f2[:, 0:N // 2].bitcast(mybir.dt.int16)
        raised = t_f2[:, N // 2:N].bitcast(BF16)
        junk = [t_a2[:, :].bitcast(BF16)[:, 0:max(b - a for a, b in PARTS[n]) * 8 * CHUNKS[n]].rearrange("p (t c) -> p t c", c=8 * CHUNKS[n])
                for n in range(STEPS)]
        w31s = sb("w31s", [D, 2 * DA])
        w2s = sb("w2s", [2 * DA, DA])[DA:, :]
        us = sb("us", [P, 2 * STEPS, D])
        wrs = sb("wrs", [D, E])
        brs = sb("brs", [P, E])
        gs = sb("gs", [P, D])
        bs = sb("bs", [P, D])
        cs = sb("cs", [P, 3 * P + E + 1])
        ident, tri, ones = cs[:, 0:P], cs[:, P:2 * P], cs[:, 2 * P:3 * P]
        iota = cs[:, 3 * P:3 * P + E]
        real = cs[:, 3 * P + E:3 * P + E + 1]
        stats = sb("stats", [P, T, 6])
        mv = sb("mv", [P, T, 2])
        rstd = sb("rstd", [P, T])
        etop = sb("etop", [P, T, 8])
        negmax = sb("negmax", [P, T])
        cum = sb("cum", [P, T, 9])
        done8 = sb("done8", [P, T, 8])
        work8 = sb("work8", [P, T, 8])
        zsum = sb("zsum", [P, T])
        target = sb("target", [P, T])
        lo = sb("lo", [P, T])
        hi = sb("hi", [P, T])
        mid = sb("mid", [P, T])
        mass = sb("mass", [P, T])
        above = sb("above", [P, T])
        found = sb("found", [P, T])
        hidden = sb("hidden", [P, T])
        one_i = sb("one_i", [P, T], I32)
        last7 = sb("last7", [P, T, 7])
        place = sb("place", [P, T, 8], U32)
        retop = sb("retop", [P, 1, 8])
        redone = sb("redone", [P, 1, 8])
        both = sb("both", [P, 2, T])
        both_i = sb("both_i", [1, 2, T], I32)
        some_i = sb("some_i", [1, 2], I32)
        some = sb("some", [1, 2])
        flags, ties = both[:, 0, :], both[:, 1, :]
        opened = sb("opened", [P, 1], U32)
        flag32 = sb("flag32", [P, 32])
        flag32t = sb("flag32t", [P, 32])
        low_i = sb("low_i", [P, T], I32)
        high_i = sb("high_i", [P, T], I32)
        yes = sb("yes", [P, T], U32)
        no = sb("no", [P, T], U32)
        cut = sb("cut", [P, T])
        flag1 = sb("flag1", [P, 1])
        flag_i = sb("flag_i", [P, 1], I32)
        kept = sb("kept", [P, T])
        rkept = sb("rkept", [P, T])
        rrow = sb("rrow", [P, T])
        rinv = sb("rinv", [P, T])

        flat_p = probs[:, :, :].rearrange("p t n -> p (t n)")
        xg = flat_p[0:CAP, 0:E * D].rearrange("p (e d) -> p e d", e=E)
        xgt = flat_p[:, E * D:E * D + E * CAP].rearrange("p (e c) -> p e c", e=E)
        late = flat_p[:, E * D + E * CAP:E * D + E * CAP + 2 * D].rearrange("p (k d) -> p k d", k=2)
        eb1s, eb2s = late[:, 0, :], late[0:E, 1, :]
        zero = a1[:, 0:8, :]
        flat_s = adj[:, :, :].rearrange("p t n -> p (t n)")
        at = 0

        def region(n):
            nonlocal at
            at += n
            return flat_s[:, at - n:at]

        rw1 = region(SLOTS * F).rearrange("p (s f) -> p s f", s=SLOTS)
        rw2 = region(SLOTS * FC * D).rearrange("p (s c d) -> p s c d", s=SLOTS, c=FC)
        ysb = region(SLOTS * D).rearrange("p (s d) -> p s d", s=SLOTS)
        yg = region(2 * T * D).rearrange("p (k t d) -> p k t d", k=2, t=T)
        hid = region(2 * FC * P).rearrange("p (b c n) -> p b c n", b=2, c=FC)
        assert at <= T * NP
        flat_pt = p_t[:, :, :, :].rearrange("p b t n -> p (b t n)")
        lg = flat_pt[:, 0:T * E].rearrange("p (t e) -> p t e", t=T)
        m1 = flat_pt[:, T * E:2 * T * E].rearrange("p (t e) -> p t e", t=T)
        m2 = flat_pt[:, 2 * T * E:3 * T * E].rearrange("p (t e) -> p t e", t=T)
        flat_f1 = f1[:, :, :].rearrange("p t n -> p (t n)")
        mm = flat_f1[:, 0:T * E].rearrange("p (t e) -> p t e", t=T)
        macc = t_a2[:, 0:(T + 1) * E].rearrange("p (t e) -> p t e", t=T + 1)
        comb = flat_pt[:, 3 * T * E:4 * T * E].rearrange("p (t e) -> p t e", t=T)
        comb_t = t_a[0:E, :]
        prod = t_f1[:, T * E:2 * T * E].rearrange("p (t e) -> p t e", t=T)
        hrow = a1
        xn = f0[:, :, 0:D]
        x1 = t_f2[:, :].rearrange("p (t d) -> p t d", t=T)
        tmp = t_a2[:, :].rearrange("p (t d) -> p t d", t=T)
        acc = a1
        flat_c = cand[:, :, :].rearrange("p t c -> p (t c)")
        used = 0

        def small(*shape, dt=F32):
            nonlocal used
            size = math.prod(shape)
            used += size
            piece = flat_c[:, used - size:used]
            piece = piece if dt is F32 else piece.bitcast(dt)
            return piece if len(shape) == 1 else piece.rearrange("p (a b) -> p a b", a=shape[0])

        top = small(T, 8)
        idx8 = small(T, 8, dt=U32)
        eidx = small(2, T)
        rank = small(2, T)
        base = small(2, T)
        ok1 = small(2, T)
        ok2 = small(2, T)
        slot = small(2, T)
        slot_i = small(2, T, dt=I32)
        gate = small(2, T)
        gdiff = small(T)
        gexp = small(T)
        most = small(1)
        most_i = small(1, dt=I32)

        psum = ctx.enter_context(nc.psum_tensor("psum", [P, 8, 512], F32))
        flat = psum[:, :, :].rearrange("p b n -> p (b n)")
        SETS = [flat[:, 0:1536], flat[:, 1536:3072]]
        counts = SETS[1][0:1, NP:NP + 2 * T].rearrange("p (k t) -> p k t", k=2)

        s_eb = sem("expert_biases_loaded")
        s_x, s_adj, s_w, s_xr = sem("x_loaded"), sem("adj_loaded"), sem("weights_loaded"), sem("x_reloaded")
        s_zero, s_zeroed = sem("zero_tile_ready"), sem("slots_zeroed")
        s_pad = sem("lower_rows_zeroed")
        s_col = sem("column_numbers_ready")
        s_flag, s_flagsum = sem("flags_ready"), sem("flags_summed")
        s_var, s_std = sem("variance_ready"), sem("std_ready")
        s_norm = sem("rows_normalised")
        KINDS = ("x", "rx", "ax", "rrx", "aax", "xn")
        s_tp = {kind: sem(f"{kind}_transposed") for kind in KINDS}
        s_te = {kind: sem(f"{kind}_transpose_copied") for kind in KINDS}
        s_proj, s_projc, s_kc = sem("projections_done"), sem("projections_copied"), sem("k_copied")
        s_lg = [sem(f"logits_ready{n}") for n in range(STEPS)]
        s_neg = [sem(f"negmax_ready{n}") for n in range(STEPS)]
        s_exp = [sem(f"exp_done{n}") for n in range(STEPS)]
        s_r = [sem(f"adj_product_ready{n}") for n in range(STEPS)]
        s_rc = [sem(f"adj_product_copied{n}") for n in range(STEPS)]
        s_rs = sem("adj_product_scaled")
        s_mask = [sem(f"kept_ready{n}") for n in range(STEPS)]
        s_scale = [sem(f"kept_scale_ready{n}") for n in range(STEPS)]
        s_pt = [sem(f"kept_transposed{n}") for n in range(STEPS)]
        s_ptc = [sem(f"kept_transpose_copied{n}") for n in range(STEPS)]
        s_a = [sem(f"attention_ready{n}") for n in range(STEPS)]
        s_ac = [sem(f"attention_copied{n}") for n in range(STEPS)]
        s_h0, s_h0c = sem("h_partial_ready"), sem("h_partial_copied")
        s_h, s_hc = sem("h_ready"), sem("h_copied")
        s_rl, s_rlc = sem("router_logits_ready"), sem("router_logits_read")
        s_gd, s_ge = sem("gate_difference_ready"), sem("gate_exp_ready")
        s_m, s_rk, s_rkc = sem("choices_ready"), sem("ranks_ready"), sem("ranks_read")
        s_cb, s_cbt, s_cbtc, s_b2 = sem("combine_ready"), sem("combine_transposed"), sem("combine_copied"), sem("bias_ready")
        s_most = sem("largest_count_ready")
        s_slot, s_sent = sem("slots_ready"), sem("tokens_sent")
        s_xg = [sem(f"tokens_loaded_{q}") for q in range(GROUPS)]
        s_wl = [sem(f"expert_weights{s}") for s in range(SLOTS)]
        s_pass = sem("wait_passed")
        s_xt, s_xtf = sem("tokens_transposed"), sem("transpose_banks_freed")
        s_hp, s_hf = sem("hidden_ready"), sem("hidden_banks_freed")
        s_y, s_yf = sem("expert_out_ready"), sem("out_banks_freed")
        s_ys = sem("expert_out_stored")
        s_left = [sem(f"out_half_{h}_freed") for h in range(2)]
        s_yg = [sem(f"outputs_gathered_{i}") for i in range(T)]
        s_acc, s_out = sem("result_ready"), sem("result_stored")
        block = ctx.enter_context(nc.Block())

        chunks = [(0, 512), (512, 512), (1024, N - 1024)]
        wide = [(0, 512), (512, 512), (1024, NP - 1024)]

        def rows(c):
            return P if c < T - 1 else LAST

        def held(eng, semaphore, value):
            eng.wait_ge(semaphore, value)
            eng.sem_inc(s_pass, 1)

        def each_round(eng, body):
            body(0)
            eng.wait_ge(s_most, 1)
            largest = eng.value_load(most_i[0:1, 0:1], min_val=0, max_val=N)
            with eng.If(largest > CAP):
                with eng.Fori(1, ROUNDS) as r:
                    with eng.If(largest > r * CAP):
                        body(r)

        @block.sync
        def _(sp):
            sp.dma_start(xraw[:, :, :], x.rearrange("(t p) d -> p t d", p=P)).then_inc(s_x, 16)
            for dst, src in ((w31s[:, DA:], w1_t), (w2s, w2_t), (w31s[:, 0:DA], w3_t), (cs, consts),
                             (wrs, wr), (brs, br), (gs, ln_g), (bs, ln_b)):
                sp.dma_start(dst[:, :], src).then_inc(s_w, 16)
            sp.dma_start(us[:, :, :], u_t.rearrange("(u d) o -> d u o", d=D)).then_inc(s_w, 16)
            sp.dma_start(adj[:, 0:T - 1, :], adj_t[0:(T - 1) * P, :].rearrange("(t p) n -> p t n", p=P)).then_inc(s_adj, 16)
            sp.dma_start(adj[0:LAST, T - 1, :], adj_t[(T - 1) * P:N, :]).then_inc(s_adj, 16)
            sp.wait_ge(s_zero, 1)
            repeats = E * CAP // P // 8
            sp.dma_start(slot_x.rearrange("(p a b) d -> p a (b d)", p=P, a=repeats),
                         zero.rearrange("p b d -> p (b d)").unsqueeze(1).broadcast_to([P, repeats, 8 * D])).then_inc(s_zeroed, 16)
            sp.wait_ge(s_tp["rrx"], NB)
            sp.dma_start(xraw[:, :, :], x.rearrange("(t p) d -> p t d", p=P)).then_inc(s_xr, 16)
            sp.wait_ge(s_pt[1], T)
            for dst, src in ((eb1s, eb1), (eb2s, eb2)):
                sp.dma_start(dst, src).then_inc(s_eb, 16)

            def body(r):
                def group(g):
                    for s in range(SLOTS):
                        e = g * SLOTS + s
                        sp.wait_ge(s_y, r * E + e + 1)
                        sp.dma_start(rw1[:, s, :], ew1[bass.ds(e * D, D), :]).then_inc(s_wl[s], 16)
                        sp.dma_start(rw2[:, s, :, :], ew2[bass.ds(e * F, F), :].rearrange("(c p) d -> p c d", p=P)).then_inc(s_wl[s], 16)
                with sp.Fori(0, GROUPS) as g:
                    group(g)
            each_round(sp, body)
            sp.wait_ge(s_acc, 1)
            sp.dma_start(out[0:(T - 1) * P, :].rearrange("(t p) d -> p t d", p=P), acc[:, 0:T - 1, :]).then_inc(s_out, 16)
            sp.dma_start(out[(T - 1) * P:N, :], acc[0:LAST, T - 1, :]).then_inc(s_out, 16)
            sp.wait_ge(s_out, 32)

        @block.gpsimd
        def _(gp):
            nc.gpsimd.memset(zero, 0.0).then_inc(s_zero, 1)
            gp.iota(column, pattern=[[1, N]], base=0, channel_multiplier=0, allow_small_or_imprecise_dtypes=True).then_inc(s_col, 1)
            gp.wait_ge(s_zeroed, 16)

            def body(r):
                for k in range(2):
                    held(gp, s_slot, 2 * r + k + 1)
                    for i in range(T):
                        gp.indirect_dma_start(out=slot_x, out_offset=bass.IndirectOffsetOnAxis(ap=slot_i[:, k, i:i + 1], axis=0),
                                              in_=xn[:, i, :], in_offset=None, bounds_check=E * CAP - 1, oob_is_err=False).then_inc(s_sent, 16)
                for q in range(2 * GROUPS):
                    held(gp, s_yf, r * E + (q + 1) * HALF + 2)
                    gp.dma_start(slot_y[q * HALF * CAP:(q + 1) * HALF * CAP, :].rearrange("(e c) d -> c e d", c=CAP),
                                 ysb[0:CAP, q % 2 * HALF:(q % 2 + 1) * HALF, :]).then_inc(s_ys, 16)
                    gp.wait_ge(s_ys, r * (2 * GROUPS * 16) + (q + 1) * 16)
                    gp.sem_inc(s_left[q % 2], 1)
                for i in range(T):
                    for k in range(2):
                        gp.indirect_dma_start(out=yg[:, k, i, :], out_offset=None, in_=slot_y,
                                              in_offset=bass.IndirectOffsetOnAxis(ap=slot_i[:, k, i:i + 1], axis=0),
                                              bounds_check=E * CAP - 1, oob_is_err=False).then_inc(s_yg[i], 16)
            each_round(gp, body)

        @block.tensor
        def _(pe):
            def transposes(src, which, kind, c):
                for i in range(*BANK_TILES[c]):
                    last = nc.tensor.transpose(SETS[which][0:D, i * P:(i + 1) * P], src[:, i, 0:D], ident)
                last.then_inc(s_tp[kind], 1)

            def stay_awake(count):
                for _ in range(count):
                    nc.tensor.matmul(psum[:, 7, 0:3 * P + E], ident, cs[:, 0:3 * P + E], start=True, stop=True)

            def adj_product(n, i):
                if i == 0:
                    if n == 0:
                        pe.wait_ge(s_adj, 32)
                    else:
                        pe.wait_ge(s_rs, 1)
                fin = f0 if n == 0 else f1
                if i >= 2:
                    pe.wait_ge(s_rc[n], i - 1)
                ob = psum[:, 6 + i % 2, 0:D + 1]
                for c in range(T):
                    nc.tensor.matmul(ob, adj[0:rows(c), c, i * P:(i + 1) * P], fin[0:rows(c), c, 0:D + 1], start=(c == 0), stop=False)
                nc.tensor.matmul(ob, ident, fin[:, i, 0:D + 1], start=False, stop=True).then_inc(s_r[n], 1)

            pe.wait_ge(s_w, 16 * 9)
            pe.wait_ge(s_norm, 1)
            for c in range(NB):
                transposes(f0, 0, "x", c)
            for n in range(STEPS):
                for c, (c0, w) in enumerate(wide):
                    pe.wait_ge(s_te["x" if n == 0 else "ax"], c + 1)
                    nc.tensor.matmul(SETS[1][:, c0:c0 + w], w31s[:, :], t_a[:, c0:c0 + w], start=True, stop=True).then_inc(s_proj, 1)
                for c, (c0, w) in enumerate(wide):
                    pe.wait_ge(s_projc, 2 * NB * n + c + 1)
                    nc.tensor.matmul(SETS[0][0:DA, c0:c0 + w], w2s, t_a2[DA:2 * DA, c0:c0 + w], start=True, stop=True).then_inc(s_proj, 1)
                pe.wait_ge(s_projc, 2 * NB * (n + 1))
                pe.wait_ge(s_kc, NB * (n + 1))
                k_rows = P if n == 0 else DA
                if n == 0:
                    pe.wait_ge(s_pad, 1)
                for i in range(T):
                    if i >= 2:
                        pe.wait_ge(s_exp[n], i - 1)
                    for c0, w in chunks:
                        last = nc.tensor.matmul(SETS[i % 2][:, c0:c0 + w], q_k[0][0:k_rows, i * P:(i + 1) * P], q_k[1][0:k_rows, c0:c0 + w], start=True, stop=True)
                    last.then_inc(s_lg[n], 1)
                    for k in BETWEEN[n][i]:
                        adj_product(n, k)
                for k in range(sum(map(len, BETWEEN[n])), T):
                    adj_product(n, k)
                pe.wait_ge(s_rc[n], T)
                pe.wait_ge(s_exp[n], T)
                if n == 1:
                    nc.tensor.drain().then_inc(s_y, SLOTS)
                    for c in range(NB):
                        transposes(xraw, 0, "rrx", c)
                    pe.wait_ge(s_te["rrx"], NB)
                    for i in range(T):
                        if i >= 2:
                            pe.wait_ge(s_h0c, i - 1)
                        ob = psum[:, 6 + i % 2, 0:D]
                        for k, (u, src) in enumerate(((0, t_f1), (1, rrx_t), (2, t_a))):
                            nc.tensor.matmul(ob, src[:, i * P:(i + 1) * P], us[:, u, :], start=(k == 0), stop=False)
                        nc.tensor.matmul(ob, ident, f0[:, i, 0:D], start=False, stop=True).then_inc(s_h0, 1)
                    pe.wait_ge(s_h0c, T)
                vin = f0 if n == 0 else a1
                p1, kind = PARTS[n][1][0], ("ax", "aax")[n]

                def attention(j):
                    pe.wait_ge(s_ptc[n], j + 1)
                    if j >= 2:
                        pe.wait_ge(s_ac[n], j - 1)
                    for c in range(T):
                        last = nc.tensor.matmul(psum[:, 6 + j % 2, 0:D], p_t[0:rows(c), j % 2, c, :], vin[0:rows(c), c, 0:D], start=(c == 0), stop=(c == T - 1))
                    last.then_inc(s_a[n], 1)

                for i in range(T + 1):
                    if i == p1:
                        attention(i - 1)
                        if n == 0:
                            pe.wait_ge(s_rs, 1)
                            for c in range(NB):
                                transposes(f1, 0, "rx", c)
                        pe.wait_ge(s_ac[n], BANK_TILES[0][1])
                        transposes((a1, f1)[n], 1, kind, 0)
                    for part, (a, b) in enumerate(PARTS[n]):
                        if i == a:
                            pe.wait_ge(s_flag, n * len(PARTS[n]) + part + 1)
                            for k in range(2):
                                last = nc.tensor.matmul(counts[:, k, a:b], ones[:, 0:1], both[:, k, a:b], start=True, stop=True)
                            last.then_inc(s_flagsum, 1)
                            if i == 0:
                                stay_awake(3)
                    if i == p1:
                        pe.wait_ge(s_te[kind], 1)
                        if n == 0:
                            pe.wait_ge(s_te["rx"], NB)
                    if i < T:
                        pe.wait_ge(s_mask[n], i + 1)
                        if i >= 2:
                            pe.wait_ge(s_ptc[n], i - 1)
                        for c in range(T):
                            last = nc.tensor.transpose(SETS[i % 2][0:rows(c), c * P:(c + 1) * P], probs[:, i, c * P:c * P + rows(c)], ident)
                        last.then_inc(s_pt[n], 1)
                    if i >= 1 and i != p1:
                        attention(i - 1)
                for c in range(1, NB + n):
                    if c < NB:
                        pe.wait_ge(s_ac[n], BANK_TILES[c][1])
                        if c == 1:
                            pe.wait_ge(s_ptc[n], T)
                        transposes((a1, f1)[n], 1, kind, c)
                    if n == 1:
                        pe.wait_ge(s_te["aax"], c)
                        for i in range(*BANK_TILES[c - 1]):
                            if i >= 2:
                                pe.wait_ge(s_hc, i - 1)
                            else:
                                pe.wait_ge(s_ac[n], T)
                            ob = psum[:, 6 + i % 2, 0:D]
                            nc.tensor.matmul(ob, t_a[:, i * P:(i + 1) * P], us[:, 3, :], start=True, stop=False)
                            nc.tensor.matmul(ob, ident, f0[:, i, 0:D], start=False, stop=True).then_inc(s_h, 1)
            for c in range(NB + 1):
                if c < NB:
                    pe.wait_ge(s_norm, 2 + c)
                    transposes(xn, 0, "xn", c)
                if c >= 1:
                    pe.wait_ge(s_te["xn"], c)
                    for i in range(*BANK_TILES[c - 1]):
                        last = nc.tensor.matmul(SETS[1][:, i * E:(i + 1) * E], t_a[:, i * P:(i + 1) * P], wrs[:, :], start=True, stop=True, skip_group_check=True)
            last.then_inc(s_rl, 1)
            pe.wait_ge(s_m, 1)
            for a, b in ((0, BANK // E), (BANK // E, T)):
                ob = SETS[0][:, a * E:b * E]
                nc.tensor.matmul(ob, tri, mm[:, a:b, :], start=True, stop=False)
                nc.tensor.matmul(ob, ones, macc[:, a:b, :], start=False, stop=True)
            nc.tensor.matmul(SETS[0][:, T * E:(T + 1) * E], ones, macc[:, T, :], start=True, stop=True).then_inc(s_rk, 1)
            pe.wait_ge(s_cb, 1)
            pe.wait_ge(s_rlc, 1)
            for i in range(T):
                last = nc.tensor.transpose(SETS[1][0:E, i * P:(i + 1) * P], comb[:, i, :], ident)
            last.then_inc(s_cbt, 1)
            pe.wait_ge(s_cbtc, 1)
            pe.wait_ge(s_rkc, 2)
            pe.wait_ge(s_eb, 32)
            for i in range(T):
                last = nc.tensor.matmul(SETS[0][:, i * D:(i + 1) * D], comb_t[:, i * P:(i + 1) * P], eb2s, start=True, stop=True)
            last.then_inc(s_b2, 1)

            def body(r):
                held(pe, s_sent, (r + 1) * (2 * T * 16))
                stay_awake(4)
                for b in range(E // 4):
                    if b * 4 % SLOTS == 0:
                        held(pe, s_xg[b * 4 // SLOTS], (r + 1) * 16)
                    pe.wait_ge(s_xtf, r * (E // 4) + b + 1)
                    for k in range(4):
                        last = nc.tensor.transpose(psum[:, b % 2, k * CAP:(k + 1) * CAP], xg[:, 4 * b + k, :], ident[0:CAP, 0:CAP])
                    last.then_inc(s_xt, 1)
                held(pe, s_xtf, (r + 1) * (E // 4) + 2)

                def first(e, s, loads):
                    held(pe, s_wl[s], 32 * (r * GROUPS + loads))
                    pe.wait_ge(s_hf, r * E + e + 1)
                    for c in range(FC):
                        last = nc.tensor.matmul(psum[:, 2 + s % 2, c * CAP:(c + 1) * CAP], rw1[:, s, c * P:(c + 1) * P],
                                                xgt[:, bass.ds(e, 1), :], start=True, stop=True)
                    last.then_inc(s_hp, 1)

                def second(e, s):
                    pe.wait_ge(s_hf, r * E + e + 3)
                    pe.wait_ge(s_yf, r * E + e + 1)
                    for c in range(FC):
                        last = nc.tensor.matmul(psum[0:CAP, 4 + s % 2, 0:D], hid[:, s % 2, c, 0:CAP], rw2[:, s, c, :],
                                                start=(c == 0), stop=(c == FC - 1))
                    last.then_inc(s_y, 1)

                first(0, 0, 1)
                with pe.Fori(0, GROUPS - 1) as g:
                    for s in range(SLOTS):
                        first(g * SLOTS + s + 1, (s + 1) % SLOTS, g + (1 if s < SLOTS - 1 else 2))
                        second(g * SLOTS + s, s)
                for s in range(SLOTS):
                    if s < SLOTS - 1:
                        first(E - SLOTS + s + 1, s + 1, GROUPS)
                    second(E - SLOTS + s, s)
            each_round(pe, body)

        @block.scalar
        def _(act):
            def std(k):
                act.wait_ge(s_var, k)
                nc.scalar.activation(rstd[:, :], rstd[:, :], ACT.Sqrt).then_inc(s_std, 1)

            def copy_bank(dst, which, kind, c):
                c0, w = wide[c]
                act.wait_ge(s_tp[kind], c + 1)
                nc.scalar.activation(dst[:, c0:c0 + w], SETS[which][:, c0:c0 + w], ACT.Copy).then_inc(s_te[kind], 1)

            def copy_out(dst, which, kind):
                for c in range(NB):
                    copy_bank(dst, which, kind, c)

            def adj_copy(n, i):
                if n == 1 and i == 0:
                    act.wait_ge(s_rs, 1)
                act.wait_ge(s_r[n], i + 1)
                if n == 0:
                    nc.scalar.activation(rrow[:, i:i + 1], psum[:, 6 + i % 2, D:D + 1], ACT.Copy)
                scale = {} if n == 0 else dict(scale=rinv[:, i:i + 1])
                nc.scalar.activation((f1, xraw)[n][:, i, 0:D], psum[:, 6 + i % 2, 0:D], ACT.Copy, **scale).then_inc(s_rc[n], 1)

            std(1)
            copy_out(t_a, 0, "x")
            for n in range(STEPS):
                for k, (dst, src) in enumerate(((t_a2[DA:2 * DA, :], SETS[1][DA:2 * DA, :]), (q_t, SETS[0][0:DA, :]))):
                    for c, (c0, w) in enumerate(wide):
                        act.wait_ge(s_proj, NB * (2 * n + k) + c + 1)
                        nc.scalar.activation(dst[:, c0:c0 + w], src[:, c0:c0 + w], ACT.Copy).then_inc(s_projc, 1)
                for i in range(T):
                    act.wait_ge(s_neg[n], i + 1)
                    nc.scalar.activation(probs[:, i, :], SETS[i % 2][:, 0:N], ACT.Exp, bias=negmax[:, i:i + 1],
                                         accum_out=zsum[:, i:i + 1])
                    nc.scalar.activation(cand[:, i, 0:8 * CHUNKS[n]], cand[:, i, 0:8 * CHUNKS[n]], ACT.Exp, bias=negmax[:, i:i + 1]).then_inc(s_exp[n], 1)
                    for k in BETWEEN[n][i]:
                        adj_copy(n, k)
                for k in range(sum(map(len, BETWEEN[n])), T):
                    adj_copy(n, k)
                if n == 1:
                    copy_out(rrx_t, 0, "rrx")
                    for i in range(T):
                        act.wait_ge(s_h0, i + 1)
                        nc.scalar.activation(f0[:, i, 0:D], psum[:, 6 + i % 2, 0:D], ACT.Copy).then_inc(s_h0c, 1)
                adst = a1 if n == 0 else f1
                if n == 0:
                    act.wait_ge(s_zeroed, 16)
                p1, kind = PARTS[n][1][0], ("ax", "aax")[n]

                def attention_copy(j):
                    act.wait_ge(s_a[n], j + 1)
                    act.wait_ge(s_scale[n], j + 1)
                    nc.scalar.activation(adst[:, j, 0:D], psum[:, 6 + j % 2, 0:D], ACT.Copy, scale=rkept[:, j:j + 1]).then_inc(s_ac[n], 1)

                for i in range(T + 1):
                    if i == p1:
                        attention_copy(i - 1)
                        if n == 0:
                            copy_out(t_f1, 0, "rx")
                        copy_bank(t_a, 1, kind, 0)
                    if i < T:
                        act.wait_ge(s_pt[n], i + 1)
                        if i >= 2:
                            act.wait_ge(s_a[n], i - 1)
                        pt = p_t[:, i % 2, :, :].rearrange("p t n -> p (t n)")
                        nc.scalar.activation(pt[:, 0:NP - P], SETS[i % 2][:, 0:NP - P], ACT.Copy)
                        nc.scalar.activation(pt[0:LAST, NP - P:NP], SETS[i % 2][0:LAST, NP - P:NP], ACT.Copy).then_inc(s_ptc[n], 1)
                    if i >= 1 and i != p1:
                        attention_copy(i - 1)
                if n == 0:
                    for c in range(1, NB):
                        copy_bank(t_a, 1, kind, c)
            for c in range(1, NB + 1):
                if c < NB:
                    copy_bank(t_a, 1, "aax", c)
                for i in range(*BANK_TILES[c - 1]):
                    act.wait_ge(s_h, i + 1)
                    nc.scalar.activation(hrow[:, i, :], psum[:, 6 + i % 2, 0:D], ACT.Copy).then_inc(s_hc, 1)
            std(2)
            std(3)
            copy_out(t_a, 0, "xn")
            act.wait_ge(s_gd, 1)
            nc.scalar.activation(gexp, gdiff, ACT.Exp).then_inc(s_ge, 1)
            act.wait_ge(s_cbt, 1)
            nc.scalar.activation(comb_t[:, :], SETS[1][0:E, 0:NP], ACT.Copy).then_inc(s_cbtc, 1)
            act.wait_ge(s_eb, 32)
            nc.scalar.drain().then_inc(s_hf, 2)
            nc.scalar.drain().then_inc(s_left[0], 1)
            nc.scalar.drain().then_inc(s_left[1], 1)

            def body(r):
                held(act, s_sent, (r + 1) * (2 * T * 16))
                for q in range(GROUPS):
                    act.dma_start(xg[:, q * SLOTS:(q + 1) * SLOTS, :],
                                  slot_x[q * SLOTS * CAP:(q + 1) * SLOTS * CAP, :].rearrange("(e c) d -> c e d", c=CAP)).then_inc(s_xg[q], 16)

                def group(g):
                    for s in range(SLOTS):
                        e = g * SLOTS + s
                        act.wait_ge(s_hp, r * E + e + 1)
                        if s >= 2:
                            act.wait_ge(s_y, SLOTS + r * E + e - 1)
                        for c in range(FC):
                            last = nc.scalar.activation(hid[:, s % 2, c, 0:CAP], psum[:, 2 + s % 2, c * CAP:(c + 1) * CAP], ACT.Relu,
                                                        bias=eb1s[:, bass.ds(e * FC + c, 1)])
                        last.then_inc(s_hf, 1)
                with act.Fori(0, GROUPS) as g:
                    group(g)
            each_round(act, body)

        @block.vector
        def _(dve):
            V = nc.vector

            def settle():
                V.drain()

            def aggregate():
                settle()
                for i in range(T):
                    V.bn_aggr(mv[:, i, :], stats[:, i, :])
                settle()
                V.tensor_scalar(rstd[:, :], mv[:, :, 1], EPS, None, ALU.add).then_inc(s_var, 1)

            def invert_std(k):
                dve.wait_ge(s_std, k)
                V.reciprocal(rstd[:, :], rstd[:, :])
                settle()

            def variance(src, k):
                for i in range(T):
                    V.bn_stats(stats[:, i, :], src(i))
                aggregate()
                invert_std(k)

            def normalise(src, dst, k):
                variance(src, k)
                for i in range(T):
                    V.tensor_scalar(dst(i), src(i), mv[:, i, 0:1], rstd[:, i:i + 1], ALU.subtract, ALU.mult)
                settle()

            V.memset(f0[:, :, D:D + 1], 1.0)
            V.memset(p_t[DA:P, :, :, :], 0.0).then_inc(s_pad, 1)
            dve.wait_ge(s_x, 16)
            normalise(lambda i: xraw[:, i, :], lambda i: f0[:, i, 0:D], 1)
            V.memset(f1[:, :, D:D + 1], 1.0)
            V.drain().then_inc(s_norm, 1)

            def cumulate(a, b, eight):
                for j in range(8):
                    V.tensor_tensor(cum[:, a:b, j + 1], cum[:, a:b, j], eight[:, :, j], ALU.add)
                    settle()

            def update(a, b):
                V.tensor_tensor(yes[:, a:b], mass[:, a:b], target[:, a:b], ALU.is_lt)
                V.tensor_tensor(no[:, a:b], mass[:, a:b], target[:, a:b], ALU.is_ge)
                settle()
                V.copy_predicated(hi[:, a:b], yes[:, a:b], mid[:, a:b])
                V.copy_predicated(above[:, a:b], yes[:, a:b], mass[:, a:b])
                V.copy_predicated(lo[:, a:b], no[:, a:b], mid[:, a:b])
                settle()

            def row_mass(i):
                V.scalar_tensor_tensor(out=below[:, :], in0=probs[:, i, :], scalar=mid[:, i:i + 1], in1=probs[:, i, :],
                                       op0=ALU.is_ge, op1=ALU.mult, accum_out=mass[:, i:i + 1])
                settle()

            def halve_row(i):
                lo_i, hi_i, mid_i = (a[:, i:i + 1].bitcast(I32) for a in (lo, hi, mid))
                V.tensor_tensor(low_i[:, i:i + 1], lo_i, hi_i, ALU.bitwise_xor)
                V.tensor_tensor(high_i[:, i:i + 1], lo_i, hi_i, ALU.bitwise_and)
                settle()
                V.tensor_scalar(low_i[:, i:i + 1], low_i[:, i:i + 1], 1, None, ALU.arith_shift_right)
                settle()
                V.tensor_tensor(mid_i, low_i[:, i:i + 1], high_i[:, i:i + 1], ALU.add)
                settle()
                row_mass(i)
                update(i, i + 1)

            def read_cut(a, b, to, eight, d, w):
                V.tensor_copy(cum[:, a:b, 0], above[:, a:b])
                settle()
                cumulate(a, b, eight)
                V.tensor_tensor(d, cum[:, a:b, 0:8], target[:, a:b].unsqueeze(2).broadcast_to([P, b - a, 8]), ALU.is_ge)
                settle()
                V.scalar_tensor_tensor(out=w, in0=d, scalar=4.0, in1=eight, op0=ALU.mult, op1=ALU.add)
                settle()
                V.tensor_reduce(to[:, a:b], w, axis=AX.X, op=ALU.min)
                settle()
                V.tensor_tensor(w, d, eight, ALU.mult)
                settle()
                V.tensor_reduce(mass[:, a:b], w, axis=AX.X, op=ALU.max)
                settle()
                V.tensor_tensor(mass[:, a:b], mass[:, a:b], to[:, a:b], ALU.is_ge)
                V.tensor_scalar(flags[:, a:b], d[:, :, 7], -1.0, 1.0, ALU.mult, ALU.add)
                settle()

            def any_flag(flags, a, b):
                V.tensor_reduce(flag32[:, 0:1], flags[:, a:b], axis=AX.X, op=ALU.max)
                settle()
                V.transpose(flag32t[:, :], flag32[:, :])
                settle()
                V.tensor_reduce(flag1[:, :], flag32t[:, :], axis=AX.X, op=ALU.max)
                settle()
                V.tensor_copy(flag_i[:, :], flag1[:, :])
                settle()
                four = [dve.value_load(flag_i[q:q + 1, 0:1], min_val=0, max_val=2) for q in range(0, P, 32)]
                return four[0] + four[1] + four[2] + four[3]

            def exact_row(i, scan):
                one = slice(i, i + 1)
                V.tensor_scalar(lo[:, one], zsum[:, one], (1.0 - TOP_P) / (2 * N), None, ALU.mult)
                V.memset(hi[:, one], 2.0)
                V.memset(above[:, one], 0.0)
                settle()
                with dve.Fori(0, EXACT):
                    halve_row(i)
                V.tensor_copy(cut[:, one], lo[:, one])
                V.tensor_tensor(mass[:, one], target[:, one], above[:, one], ALU.subtract)
                V.reciprocal(kept[:, one], lo[:, one])
                settle()
                V.tensor_tensor(mass[:, one], mass[:, one], kept[:, one], ALU.mult)
                settle()
                V.tensor_scalar(mass[:, one], mass[:, one], 1.0, None, ALU.add)
                V.tensor_scalar(below[:, :], probs[:, i, :], cut[:, one], None, ALU.is_equal)
                settle()
                V.tensor_tensor_scan(scan, below[:, :], below[:, :], 0.0, ALU.add, ALU.max)
                settle()
                V.tensor_tensor(below[:, :], below[:, :], scan, ALU.mult)
                settle()
                V.scalar_tensor_tensor(out=probs[:, i, :], in0=below[:, :], scalar=mass[:, one], in1=probs[:, i, :],
                                       op0=ALU.is_lt, op1=ALU.mult)
                V.memset(ties[:, one], 0.0)
                settle()

            def retry_row(i, scan):
                one = slice(i, i + 1)
                V.tensor_copy(opened[:, :], flags[:, one])
                V.tensor_tensor(yes[:, one], hidden[:, one], cut[:, one], ALU.is_ge)
                V.memset(redone[:, 0, 0:1], 2.0)
                V.memset(redone[:, 0, 1:2], 0.0)
                V.tensor_scalar(mid[:, one], hidden[:, one], 1.0 + 2.0 ** -20, None, ALU.mult)
                settle()
                V.copy_predicated(hi[:, one], yes[:, one], redone[:, 0, 0:1])
                V.copy_predicated(above[:, one], yes[:, one], redone[:, 0, 1:2])
                V.tensor_tensor(mid[:, one], mid[:, one], lo[:, one], ALU.max)
                settle()
                row_mass(i)
                update(i, i + 1)
                with dve.Fori(0, RETRY):
                    halve_row(i)
                V.scalar_tensor_tensor(out=below[:, :], in0=probs[:, i, :], scalar=hi[:, one], in1=probs[:, i, :],
                                       op0=ALU.is_lt, op1=ALU.mult)
                settle()
                V.max(retop[:, 0, :], below[:, :])
                settle()
                read_cut(i, i + 1, found, retop[:, :, :], redone[:, :, :], work8[:, i:i + 1, :])
                V.copy_predicated(cut[:, one], opened[:, :], found[:, one])
                V.copy_predicated(ties[:, one], opened[:, :], mass[:, one])
                V.copy_predicated(etop[:, i, :], opened[:, :].broadcast_to([P, 8]), retop[:, 0, :])
                V.copy_predicated(done8[:, i, :], opened[:, :].broadcast_to([P, 8]), redone[:, 0, :])
                V.tensor_tensor(flags[:, one], flags[:, one], opened[:, :], ALU.mult)
                settle()
                with dve.If(any_flag(flags, i, i + 1) > 0):
                    exact_row(i, scan)

            V.memset(flag32[:, :], 0.0)
            V.memset(one_i[:, :], 1)
            dve.wait_ge(s_col, 1)
            for n in range(STEPS):
                width, chunk_count = WIDTH[n], CHUNKS[n]
                cands = 8 * chunk_count
                for c, (c0, w) in enumerate(wide):
                    dve.wait_ge(s_projc, 2 * NB * n + c + 1)
                    V.tensor_copy(k_t[:, c0:c0 + w], SETS[1][0:DA, c0:c0 + w]).then_inc(s_kc, 1)
                for i in range(T):
                    dve.wait_ge(s_lg[n], i + 1)
                    for c in range(chunk_count):
                        V.max(cand[:, i, 8 * c:8 * c + 8], SETS[i % 2][:, c * width:(N if c == chunk_count - 1 else (c + 1) * width)])
                    settle()
                    V.tensor_reduce(negmax[:, i:i + 1], cand[:, i, 0:cands:8], axis=AX.X, op=ALU.max)
                    settle()
                    V.tensor_scalar(negmax[:, i:i + 1], negmax[:, i:i + 1], -1.0, None, ALU.mult).then_inc(s_neg[n], 1)
                for part, (a, b) in enumerate(PARTS[n]):
                    if n == 0 and part == 1:
                        dve.wait_ge(s_rc[0], T)
                        V.reciprocal(rinv[:, :], rrow[:, :])
                        settle()
                        V.tensor_tensor(f1[:, :, 0:D], f1[:, :, 0:D], rinv[:, :].unsqueeze(2).broadcast_to([P, T, D]), ALU.mult).then_inc(s_rs, 1)
                    dve.wait_ge(s_exp[n], b)
                    V.tensor_scalar(target[:, a:b], zsum[:, a:b], TOP_P, None, ALU.mult)
                    V.tensor_scalar(lo[:, a:b], zsum[:, a:b], (1.0 - TOP_P) / (2 * N), None, ALU.mult)
                    V.memset(hi[:, a:b], 2.0)
                    V.memset(above[:, a:b], 0.0)
                    V.tensor_reduce(hidden[:, a:b], cand[:, a:b, 7:cands:8], axis=AX.X, op=ALU.max)
                    settle()
                    for k in range(STEPS_OF_CUT[n]):
                        V.tensor_scalar(mid[:, a:b], lo[:, a:b], 2.0 ** (RANGE / 2 ** (k + 1)), None, ALU.mult)
                        settle()
                        for i in range(a, b):
                            V.scalar_tensor_tensor(out=junk[n][:, i - a, :], in0=cand[:, i, 0:cands], scalar=mid[:, i:i + 1], in1=cand[:, i, 0:cands],
                                                   op0=ALU.is_ge, op1=ALU.mult, accum_out=mass[:, i:i + 1])
                        settle()
                        update(a, b)
                    for j in range(a, b, 2):
                        pair = range(j, min(j + 2, b))
                        for i in pair:
                            V.scalar_tensor_tensor(out=picked[:, i % 2, 0:cands], in0=cand[:, i, 0:cands], scalar=hi[:, i:i + 1], in1=cand[:, i, 0:cands],
                                                   op0=ALU.is_lt, op1=ALU.mult)
                        settle()
                        for i in pair:
                            V.max(etop[:, i, :], picked[:, i % 2, 0:cands])
                        settle()
                    read_cut(a, b, cut, etop[:, a:b, :], done8[:, a:b, :], work8[:, a:b, :])
                    V.tensor_copy(ties[:, a:b], mass[:, a:b])
                    settle()
                    V.tensor_tensor(mass[:, a:b], hidden[:, a:b], cut[:, a:b], ALU.is_ge)
                    settle()
                    V.tensor_tensor(flags[:, a:b], flags[:, a:b], mass[:, a:b], ALU.max).then_inc(s_flag, 1)
                    dve.wait_ge(s_flagsum, n * len(PARTS[n]) + part + 1)
                    sums = counts[:, :, a:b]
                    V.tensor_copy(both_i[:, :, a:b], sums)
                    V.tensor_reduce(some[:, :], sums, axis=AX.X, op=ALU.add)
                    settle()
                    V.tensor_copy(some_i[:, :], some[:, :])
                    settle()
                    opens = dve.value_load(some_i[0:1, 0:1], min_val=0, max_val=NP)
                    tied = dve.value_load(some_i[0:1, 1:2], min_val=0, max_val=NP)
                    scan = cand[:, a:b, :].rearrange("p t c -> p (t c)")[:, 0:N]
                    with dve.If(opens > 0):
                        for i in range(a, b):
                            with dve.If(dve.value_load(both_i[0:1, 0, i:i + 1], min_val=0, max_val=P) > 0):
                                retry_row(i, scan)
                    def scale_of(i):
                        if i >= a:
                            V.scalar_tensor_tensor(out=kept[:, i:i + 1], in0=zsum[:, i:i + 1], scalar=1e-12, in1=kept[:, i:i + 1], op0=ALU.mult, op1=ALU.max)
                        if i >= a + 1:
                            V.reciprocal(rkept[:, i - 1:i], kept[:, i - 1:i]).then_inc(s_scale[n], 1)

                    def last_scales():
                        settle()
                        scale_of(b - 1)
                        settle()
                        V.reciprocal(rkept[:, b - 1:b], kept[:, b - 1:b]).then_inc(s_scale[n], 1)

                    with dve.If(tied > 0):
                        V.tensor_tensor(high_i[:, a:b], cut[:, a:b].bitcast(I32), one_i[:, a:b], ALU.add)
                        V.tensor_tensor(last7[:, a:b, :], done8[:, a:b, 1:8], done8[:, a:b, 0:7], ALU.subtract)
                        settle()
                        V.tensor_tensor(lo[:, a:b], high_i[:, a:b].bitcast(F32), cut[:, a:b], ALU.subtract)
                        settle()
                        V.tensor_tensor(lo[:, a:b], lo[:, a:b], ties[:, a:b], ALU.mult)
                        for i in range(a, b):
                            V.max_index(place[:, i, :], etop[:, i, :], probs[:, i, :])
                        settle()
                        V.tensor_copy(work8[:, a:b, :], place[:, a:b, :])
                        settle()
                        V.tensor_tensor(work8[:, a:b, 0:7], work8[:, a:b, 0:7], last7[:, a:b, :], ALU.mult)
                        settle()
                        V.tensor_reduce(mid[:, a:b], work8[:, a:b, 0:7], axis=AX.X, op=ALU.add)
                        settle()
                        def raise_cut(i):
                            V.tensor_scalar(raised, column, mid[:, i:i + 1], lo[:, i:i + 1], ALU.is_gt, ALU.mult)

                        raise_cut(a)
                        for i in range(a, b):
                            settle()
                            V.scalar_tensor_tensor(out=below[:, :], in0=raised, scalar=cut[:, i:i + 1], in1=probs[:, i, :],
                                                   op0=ALU.add, op1=ALU.is_le)
                            scale_of(i - 1)
                            settle()
                            V.scalar_tensor_tensor(out=probs[:, i, :], in0=below[:, :], scalar=1.0, in1=probs[:, i, :],
                                                   op0=ALU.mult, op1=ALU.mult, accum_out=kept[:, i:i + 1]).then_inc(s_mask[n], 1)
                            if i + 1 < b:
                                raise_cut(i + 1)
                        last_scales()
                    with dve.Else():
                        for i in range(a, b):
                            V.scalar_tensor_tensor(out=probs[:, i, :], in0=probs[:, i, :], scalar=cut[:, i:i + 1], in1=probs[:, i, :],
                                                   op0=ALU.is_ge, op1=ALU.mult, accum_out=kept[:, i:i + 1]).then_inc(s_mask[n], 1)
                            scale_of(i - 1)
                            settle()
                        last_scales()

            dve.wait_ge(s_xr, 16)
            dve.wait_ge(s_w, 16 * 9)
            V.tensor_tensor(xraw[:, :, :], xraw[:, :, :], bs[:, :].unsqueeze(1).broadcast_to([P, T, D]), ALU.add)
            for i in range(T):
                dve.wait_ge(s_hc, i + 1)
                V.bn_stats(stats[:, i, :], hrow[:, i, :])
            aggregate()
            for i in range(T):
                V.scalar_tensor_tensor(out=tmp[:, i, :], in0=hrow[:, i, :], scalar=mv[:, i, 0:1], in1=gs[:, :], op0=ALU.subtract, op1=ALU.mult)
            invert_std(2)
            for i in range(T):
                V.scalar_tensor_tensor(out=x1[:, i, :], in0=tmp[:, i, :], scalar=rstd[:, i:i + 1], in1=xraw[:, i, :], op0=ALU.mult, op1=ALU.add)
            settle()
            variance(lambda i: x1[:, i, :], 3)
            for a, b in BANK_TILES:
                for i in range(a, b):
                    V.tensor_scalar(xn[:, i, :], x1[:, i, :], mv[:, i, 0:1], rstd[:, i:i + 1], ALU.subtract, ALU.mult)
                V.drain().then_inc(s_norm, 1)
            V.memset(yg, 0.0)
            V.memset(macc[:, 0, :], 0.0)
            dve.wait_ge(s_rl, 1)
            V.tensor_tensor(lg, SETS[1][:, 0:T * E].rearrange("p (t e) -> p t e", t=T), brs[:, :].unsqueeze(1).broadcast_to([P, T, E]), ALU.add).then_inc(s_rlc, 1)
            settle()
            for i in range(T):
                V.max(top[:, i, :], lg[:, i, :])
            settle()
            for i in range(T):
                V.max_index(idx8[:, i, :], top[:, i, :], lg[:, i, :])
            V.tensor_tensor(gdiff, top[:, :, 1], top[:, :, 0], ALU.subtract).then_inc(s_gd, 1)
            settle()
            for k in range(2):
                V.tensor_copy(eidx[:, k, :], idx8[:, :, k])
            settle()
            for k, m in enumerate((m1, m2)):
                V.tensor_tensor(m, iota.unsqueeze(1).broadcast_to([P, T, E]), eidx[:, k, :].unsqueeze(2).broadcast_to([P, T, E]), ALU.is_equal)
            settle()
            for m in (m1, m2):
                V.tensor_scalar(m[:, T - 1, :], m[:, T - 1, :], real, None, ALU.mult)
            settle()
            V.tensor_tensor(mm, m1, m2, ALU.add)
            settle()
            V.tensor_copy(macc[:, 1, :], mm[:, 0, :])
            settle()
            for i in range(1, T):
                V.tensor_tensor(macc[:, i + 1, :], macc[:, i, :], mm[:, i, :], ALU.add)
                settle()
            V.drain().then_inc(s_m, 1)
            V.tensor_scalar(flag1[:, :], real, -FAR, FAR, ALU.mult, ALU.add)
            V.tensor_scalar(base[:, :, :], eidx[:, :, :], float(CAP), -FAR, ALU.mult, ALU.add)
            settle()
            dve.wait_ge(s_rk, 1)
            V.tensor_reduce(most, SETS[0][:, T * E:(T + 1) * E], axis=AX.X, op=ALU.max)
            settle()
            V.tensor_copy(most_i, most)
            V.drain().then_inc(s_most, 1)

            def first_rank(k):
                V.tensor_tensor(prod, SETS[0][:, 0:T * E].rearrange("p (t e) -> p t e", t=T), (m1, m2)[k], ALU.mult).then_inc(s_rkc, 1)
                settle()
                V.tensor_reduce(rank[:, k, :], prod, axis=AX.X, op=ALU.add)
                settle()
                V.tensor_scalar(rank[:, k, T - 1:T], rank[:, k, T - 1:T], flag1[:, 0:1], None, ALU.add)
                settle()

            def first_sum():
                dve.wait_ge(s_ge, 1)
                V.tensor_scalar(gdiff, gexp, 1.0, None, ALU.add)
                settle()
                V.reciprocal(gate[:, 0, :], gdiff)
                settle()
                V.tensor_tensor(gate[:, 1, :], gexp, gate[:, 0, :], ALU.mult)
                settle()
                V.tensor_tensor(comb, m1, gate[:, 0, :].unsqueeze(2).broadcast_to([P, T, E]), ALU.mult)
                V.tensor_tensor(prod, m2, gate[:, 1, :].unsqueeze(2).broadcast_to([P, T, E]), ALU.mult)
                settle()
                V.tensor_tensor(comb, comb, prod, ALU.add)
                V.drain().then_inc(s_cb, 1)
                dve.wait_ge(s_b2, 1)
                V.tensor_tensor(acc[:, :, :], SETS[0][:, 0:NP].rearrange("p (t d) -> p t d", t=T), x1, ALU.add)
                settle()
                V.drain().then_inc(s_xtf, 2)
                V.drain().then_inc(s_yf, 2)


            def body(r):
                if not isinstance(r, int):
                    V.memset(yg, 0.0)
                for k in range(2):
                    if isinstance(r, int):
                        first_rank(k)
                    V.tensor_scalar(ok1[:, k, :], rank[:, k, :], 0.0, None, ALU.is_ge)
                    V.tensor_scalar(ok2[:, k, :], rank[:, k, :], float(CAP), None, ALU.is_lt)
                    V.tensor_tensor(slot[:, k, :], base[:, k, :], rank[:, k, :], ALU.add)
                    settle()
                    V.tensor_tensor(ok1[:, k, :], ok1[:, k, :], ok2[:, k, :], ALU.mult)
                    settle()
                    V.tensor_tensor(slot[:, k, :], slot[:, k, :], ok1[:, k, :], ALU.mult)
                    settle()
                    V.tensor_scalar(slot_i[:, k, :], slot[:, k, :], FAR, None, ALU.add)
                    V.tensor_scalar(rank[:, k, :], rank[:, k, :], float(-CAP), None, ALU.add)
                    V.drain().then_inc(s_slot, 1)
                if isinstance(r, int):
                    first_sum()
                for b in range(E // 4):
                    dve.wait_ge(s_xt, r * (E // 4) + b + 1)
                    V.tensor_copy(xgt[:, 4 * b:4 * b + 4, :], psum[:, b % 2, 0:4 * CAP].rearrange("p (e c) -> p e c", e=4)).then_inc(s_xtf, 1)

                def group(g):
                    for s in range(SLOTS):
                        if s % HALF == 0:
                            dve.wait_ge(s_left[s // HALF], r * GROUPS + g + 1)
                        e = g * SLOTS + s
                        dve.wait_ge(s_y, SLOTS + r * E + e + 1)
                        V.tensor_copy(ysb[0:CAP, s, :], psum[0:CAP, 4 + s % 2, 0:D]).then_inc(s_yf, 1)
                with dve.Fori(0, GROUPS) as g:
                    group(g)
                for i in range(T):
                    dve.wait_ge(s_yg[i], (r + 1) * (2 * 16))
                    for k in range(2):
                        V.scalar_tensor_tensor(out=acc[:, i, :], in0=yg[:, k, i, :], scalar=gate[:, k, i:i + 1], in1=acc[:, i, :], op0=ALU.mult, op1=ALU.add)
                        settle()
            each_round(dve, body)
            V.drain().then_inc(s_acc, 1)


def kernel(x, adj, L0_gnn_W1, L0_gnn_W2, L0_gnn_W3, L0_gnn_U1, L0_gnn_U2, L0_gnn_ln_g, L0_gnn_ln_b,
           L0_ffn_Wr, L0_ffn_br, L0_ffn_W1, L0_ffn_b1, L0_ffn_W2, L0_ffn_b2):
    import numpy as np
    import concourse.bacc as bacc
    from concourse.bass_utils import run_bass_kernel_spmd

    f = np.float32
    pad = NP - N
    consts = np.concatenate([np.eye(P, dtype=f), np.triu(np.ones((P, P), f), 1), np.ones((P, P), f),
                             np.broadcast_to(np.arange(E, dtype=f), (P, E)),
                             (np.arange(P) < LAST).astype(f)[:, None]], axis=1)
    adj = np.asarray(adj)
    x = np.asarray(x)
    arrays = {
        "x": np.concatenate([x, x[:pad]], axis=0),
        "adj_t": np.concatenate([adj.T, adj.T[:, :pad]], axis=1),
        "w1_t": np.asarray(L0_gnn_W1).T,
        "w2_t": np.asarray(L0_gnn_W2).T,
        "w3_t": np.asarray(L0_gnn_W3).T,
        "u_t": np.concatenate([np.asarray(u)[n].T for u in (L0_gnn_U1, L0_gnn_U2) for n in range(STEPS)], axis=0),
        "ln_g": np.broadcast_to(np.asarray(L0_gnn_ln_g), (P, D)),
        "ln_b": np.broadcast_to(np.asarray(L0_gnn_ln_b), (P, D)),
        "wr": np.asarray(L0_ffn_Wr),
        "br": np.broadcast_to(np.asarray(L0_ffn_br), (P, E)),
        "ew1": np.asarray(L0_ffn_W1).reshape(E * D, F),
        "eb1": np.asarray(L0_ffn_b1).reshape(E * FC, P).T,
        "ew2": np.asarray(L0_ffn_W2).reshape(E * F, D),
        "eb2": np.asarray(L0_ffn_b2),
        "consts": consts,
    }
    nc = bacc.Bacc("TRN2", target_bir_lowering=False, num_devices=1)
    arrays = {f"in_{k}": np.ascontiguousarray(v) for k, v in arrays.items()}
    args = [nc.dram_tensor(k, v.shape, mybir.dt.from_np(v.dtype), kind="ExternalInput").ap() for k, v in arrays.items()]
    out = nc.dram_tensor("out_0", (N, D), mybir.dt.float32, kind="ExternalOutput").ap()
    build(nc, *args, out)
    return run_bass_kernel_spmd(nc, [arrays], core_ids=[0]).results[0]["out_0"]
```
